# Optimizing a Trainium2 kernel written in Bass

```python
import numpy as np
import jax
import jax.numpy as jnp

def _softmax(x, axis=-1):
    return jax.nn.softmax(x, axis=axis)

def _gelu(x):
    return jax.nn.gelu(x, approximate=True)

def _silu(x):
    return jax.nn.silu(x)

def _sigmoid(x):
    return jax.nn.sigmoid(x)

def _layernorm(x, axis=-1, eps=1e-05):
    m = jnp.mean(x, axis=axis, keepdims=True)
    v = jnp.var(x, axis=axis, keepdims=True)
    return (x - m) / jnp.sqrt(v + eps)

def _scatter_add(tgt, idx, src, axis=0):
    return tgt.at[idx].add(src)

def _segment_sum(src, seg, n):
    return jax.ops.segment_sum(src, seg, n)
kernel_name = 'mk_lm_tower_d1_tok_ids1024_r4_e734ad'

def setup_inputs(seed: int=0):
    np.random.seed(seed)
    _w = jnp.asarray

    def _rec_inputs():
        import jax
        import jax.numpy as jnp
        _rk = jax.random.key(seed)
        x = jax.random.randint(jax.random.fold_in(_rk, 1), (64, 256), 0, 12564, jnp.int32)
        return x
    x = _rec_inputs()

    def _L0_tok_setup():
        import jax, jax.numpy as jnp
        import numpy as np
        VOCAB = 50257
        EMBED = 256
        key = jax.random.key(seed)
        k1, k2 = jax.random.split(key)
        x = jax.random.randint(k1, (4, 1024), 0, VOCAB, dtype=jnp.int32)
        emb = jax.random.truncated_normal(k2, -3.0, 3.0, (VOCAB, EMBED), dtype=jnp.float32)
        return {'x': x, 'embeddings': emb}
    _L0_tok_all = _L0_tok_setup()
    _L0_tok_in = {k: v for k, v in _L0_tok_all.items() if k in ('embeddings',)}
    del _L0_tok_all

    def _L0_attn_setup():
        import jax, jax.numpy as jnp
        import numpy as np
        HIDDEN = 256
        HEADS = 16
        HEAD_DIM = HIDDEN // HEADS
        B, S = (4, 512)
        key = jax.random.key(seed)
        ks = jax.random.split(key, 10)
        scale = 1.0 / np.sqrt(HIDDEN)

        def lin(k):
            return jax.random.uniform(k, (HIDDEN, HIDDEN), jnp.float32, -scale, scale)
        return {'x': jax.random.normal(ks[0], (B, S, HIDDEN), jnp.float32), 'Wq': lin(ks[1]), 'bq': jnp.zeros((HIDDEN,), jnp.float32), 'Wk': lin(ks[2]), 'bk': jnp.zeros((HIDDEN,), jnp.float32), 'Wv': lin(ks[3]), 'bv': jnp.zeros((HIDDEN,), jnp.float32), 'Wo': lin(ks[4]), 'bo': jnp.zeros((HIDDEN,), jnp.float32), 'head_mask': jnp.ones((HEADS,), jnp.float32)}
    _L0_attn_all = _L0_attn_setup()
    _L0_attn_in = {k: v for k, v in _L0_attn_all.items() if k in ('Wq', 'bq', 'Wk', 'bk', 'Wv', 'bv', 'Wo', 'bo', 'head_mask')}
    del _L0_attn_all

    def _L0_ffn_setup():
        import jax, jax.numpy as jnp
        import numpy as np
        D_MODEL = 256
        EXPERT_DIM = 128
        N_EXPERTS = 8
        TOP_K = 2

        def _sq_relu(h):
            return jnp.square(jax.nn.relu(h))
        key = jax.random.key(seed)
        ks = jax.random.split(key, 6)
        s = 0.02
        x = jax.random.normal(ks[0], (2, 512, D_MODEL), dtype=jnp.float32)
        Ws1 = jax.random.normal(ks[1], (D_MODEL, EXPERT_DIM), dtype=jnp.float32) * s
        Ws2 = jax.random.normal(ks[2], (EXPERT_DIM, D_MODEL), dtype=jnp.float32) * s
        W1 = jax.random.normal(ks[3], (N_EXPERTS, D_MODEL, EXPERT_DIM), dtype=jnp.float32) * s
        W2 = jax.random.normal(ks[4], (N_EXPERTS, EXPERT_DIM, D_MODEL), dtype=jnp.float32) * s
        Wr = jax.random.normal(ks[5], (D_MODEL, N_EXPERTS), dtype=jnp.float32) * s
        return {'x': x, 'Ws1': Ws1, 'Ws2': Ws2, 'W1': W1, 'W2': W2, 'Wr': Wr}
    _L0_ffn_all = _L0_ffn_setup()
    _L0_ffn_in = {k: v for k, v in _L0_ffn_all.items() if k in ('Ws1', 'Ws2', 'W1', 'W2', 'Wr')}
    del _L0_ffn_all
    return {'x': x, 'L0_tok_embeddings': _L0_tok_in['embeddings'], 'L0_attn_Wq': _L0_attn_in['Wq'], 'L0_attn_bq': _L0_attn_in['bq'], 'L0_attn_Wk': _L0_attn_in['Wk'], 'L0_attn_bk': _L0_attn_in['bk'], 'L0_attn_Wv': _L0_attn_in['Wv'], 'L0_attn_bv': _L0_attn_in['bv'], 'L0_attn_Wo': _L0_attn_in['Wo'], 'L0_attn_bo': _L0_attn_in['bo'], 'L0_attn_head_mask': _L0_attn_in['head_mask'], 'L0_ffn_Ws1': _L0_ffn_in['Ws1'], 'L0_ffn_Ws2': _L0_ffn_in['Ws2'], 'L0_ffn_W1': _L0_ffn_in['W1'], 'L0_ffn_W2': _L0_ffn_in['W2'], 'L0_ffn_Wr': _L0_ffn_in['Wr']}

def reference(x, L0_tok_embeddings, L0_attn_Wq, L0_attn_bq, L0_attn_Wk, L0_attn_bk, L0_attn_Wv, L0_attn_bv, L0_attn_Wo, L0_attn_bo, L0_attn_head_mask, L0_ffn_Ws1, L0_ffn_Ws2, L0_ffn_W1, L0_ffn_W2, L0_ffn_Wr):
    import jax
    import jax.numpy as jnp

    def _L0_tok_ref(x, embeddings):
        import jax, jax.numpy as jnp
        import numpy as np
        VOCAB = 50257
        EMBED = 256
        return jnp.take(embeddings, x, axis=0)

    def _L0_attn_ref(x, Wq, bq, Wk, bk, Wv, bv, Wo, bo, head_mask):
        import jax, jax.numpy as jnp
        import numpy as np
        HIDDEN = 256
        HEADS = 16
        HEAD_DIM = HIDDEN // HEADS
        B, S = (4, 512)
        b, s, _ = x.shape
        q = (x @ Wq.T + bq).reshape(b, s, HEADS, HEAD_DIM)
        k = (x @ Wk.T + bk).reshape(b, s, HEADS, HEAD_DIM)
        v = (x @ Wv.T + bv).reshape(b, s, HEADS, HEAD_DIM)
        attn = jnp.einsum('bqhd,bkhd->bhqk', q, k) / np.sqrt(HEAD_DIM).astype(np.float32)
        attn = jax.nn.softmax(attn, axis=-1)
        attn = attn * head_mask[None, :, None, None]
        out = jnp.einsum('bhqk,bkhd->bqhd', attn, v).reshape(b, s, HIDDEN)
        return out @ Wo.T + bo

    def _L0_ffn_ref(x, Ws1, Ws2, W1, W2, Wr):
        import jax, jax.numpy as jnp
        import numpy as np
        D_MODEL = 256
        EXPERT_DIM = 128
        N_EXPERTS = 8
        TOP_K = 2

        def _sq_relu(h):
            return jnp.square(jax.nn.relu(h))
        shape = x.shape
        xf = x.reshape(-1, D_MODEL)
        out_shared = _sq_relu(xf @ Ws1) @ Ws2
        logits = xf @ Wr
        top_vals, top_idx = jax.lax.top_k(logits, TOP_K)
        rw = jax.nn.softmax(top_vals.astype(jnp.float32), axis=-1).astype(x.dtype)
        onehot = jax.nn.one_hot(top_idx, N_EXPERTS, dtype=x.dtype)
        prob = jnp.einsum('tk,tke->te', rw, onehot)
        prob = jnp.trunc(prob)
        h = _sq_relu(jnp.einsum('td,edf->tef', xf, W1))
        y = jnp.einsum('tef,efd->ted', h, W2)
        out_routed = jnp.einsum('ted,te->td', y, prob)
        return (out_shared + out_routed).reshape(shape)
    h = _L0_tok_ref(x, L0_tok_embeddings)
    h = h + _L0_attn_ref(_layernorm(h, axis=-1), L0_attn_Wq, L0_attn_bq, L0_attn_Wk, L0_attn_bk, L0_attn_Wv, L0_attn_bv, L0_attn_Wo, L0_attn_bo, L0_attn_head_mask)
    h = h + _L0_ffn_ref(_layernorm(h, axis=-1), L0_ffn_Ws1, L0_ffn_Ws2, L0_ffn_W1, L0_ffn_W2, L0_ffn_Wr)
    return h

_drawn_inputs = setup_inputs


def setup_inputs(seed=0):
    import zlib

    import numpy as np

    out = dict(_drawn_inputs(seed))
    spreads = {'L0_attn_bq': (0.0, 0.8),
     'L0_attn_bk': (0.0, 0.8),
     'L0_attn_bv': (0.0, 0.1),
     'L0_attn_bo': (0.0, 0.1)}
    factors = {'L0_attn_Wq': 5.558, 'L0_attn_Wk': 5.448}
    for name, (base, spread) in spreads.items():
        noise = np.random.default_rng([zlib.crc32(name.encode()), seed]).standard_normal(out[name].shape)
        drawn = base * np.exp(spread * noise) if base else spread * noise
        out[name] = jnp.asarray(drawn.astype(out[name].dtype))
    for name, factor in factors.items():
        out[name] = (out[name] * factor).astype(out[name].dtype)
    return out
```

```python
import concourse.bass as bass
from concourse import mybir
from contextlib import ExitStack

F32 = mybir.dt.float32
BF16 = mybir.dt.bfloat16
I32 = mybir.dt.int32
ALU = mybir.AluOpType
ACT = mybir.ActivationFunctionType
AX = mybir.AxisListType

P = 128
TERMS = [(0, 0), (0, 1), (0, 2), (1, 0), (1, 1), (2, 0)]
EPS = 1e-5


def wait(eng, sem, value):
    if not isinstance(value, int) or value > 0:
        eng.wait_ge(sem, value)


def waits_apart(eng, held, *waits):
    if all(isinstance(value, int) for _, value in waits):
        for sem, value in waits:
            wait(eng, sem, value)
    else:
        waits = [(sem, eng.to_reg(value)) for sem, value in waits]
        eng.wait_ge(*held)
        for sem, value in waits:
            eng.wait_ge(sem, value)


def tower(nc, ids, emb, wq, bq, wk, bk, wv, bv, wo, bo, mask, ws1, ws2, w1, w2, wr, out):
    SEQS, TOK, D = out.shape
    HEADS = 16
    HD = D // HEADS
    CH = TOK // P
    DC = D // P
    HC = P // HD
    GH = 4
    F = ws1.shape[1]
    EXPERTS = wr.shape[1]
    ROWS = len(TERMS) * HD
    SROWS = ROWS + 2
    W = DC * TOK

    ctx = ExitStack()
    with ctx:
        def sb(name, shape, dt=F32):
            return ctx.enter_context(nc.sbuf_tensor(name, shape, dt))

        def bank(name):
            return ctx.enter_context(nc.psum_tensor(name, [P, W], F32))

        def sem(name):
            return ctx.enter_context(nc.semaphore(name))

        parts_dram = nc.dram_tensor("parts_dram", [2, 3, D, TOK], BF16, kind="Internal").ap()
        max_dram = nc.dram_tensor("max_dram", [2, 2, HEADS // 2 * TOK], BF16, kind="Internal").ap()
        z_dram = nc.dram_tensor("z_dram", [SEQS, TOK, D], F32, kind="Internal").ap()

        ident = sb("ident", [P, P])
        ids_sb = sb("ids_sb", [P, SEQS * CH], I32)
        ids_now = sb("ids_now", [P, CH], I32)
        wq_sb, wk_sb, wv_sb, wo_sb, wo_raw = (sb(n, [P, DC, D]) for n in ("wq_sb", "wk_sb", "wv_sb", "wo_sb", "wo_raw"))
        bqk = sb("bqk", [P, 2 * DC])
        bv_sb = sb("bv_sb", [P, D])
        bo_sb = sb("bo_sb", [P, D])
        mask_sb = sb("mask_sb", [P, DC])
        ws1_sb = sb("ws1_sb", [P, DC, F])
        ws2_sb = sb("ws2_sb", [P, D])
        wr_sb = sb("wr_sb", [P, DC, EXPERTS])
        minus_half = sb("minus_half", [P, CH])

        x = sb("x", [P, 3, CH, D])
        stat1, mv1 = sb("stat1", [P, CH, 6]), sb("mv1", [P, CH, 2])
        rs1 = sb("rs1", [P, 5, CH])
        xn = sb("xn", [P, CH, D])
        xT = sb("xT", [P, DC, TOK])
        qk = sb("qk", [P, 2, DC, TOK])
        qk_rest = sb("qk_rest", [P, 2, DC, TOK])
        parts = sb("parts", [P, 2, 3, DC, TOK], BF16)
        stack_q = [sb(f"stack_q{i}", [P, HEADS, TOK], BF16) for i in range(3)]
        stack_k = [sb(f"stack_k{i}", [P, HEADS, TOK], BF16) for i in range(3)]
        v = sb("v", [P, 3, CH, HEADS, 2 * HD])
        neg_max = [sb(f"neg_max{u}", [P, P]) for u in range(2)]
        max_parts = [sb(f"max_parts{u}", [HEADS, 2, P], BF16) for u in range(2)]
        probs = sb("probs", [P, 8, CH, TOK])
        oT = sb("oT", [P, HEADS // GH, TOK])
        inv_sum = sb("inv_sum", [P, CH, HEADS])
        o_nat = sb("o_nat", [P, CH, HEADS, HD])
        o_turned = sb("o_turned", [P, DC, TOK])
        xb = sb("xb", [P, 3, CH, D])
        h1 = sb("h1", [P, CH, D])
        stat2, mv2 = sb("stat2", [P, CH, 6]), sb("mv2", [P, CH, 2])
        rs2 = sb("rs2", [P, 5, CH])
        z = sb("z", [P, CH, D])
        zT = sb("zT", [P, DC, TOK])
        hid_relu = sb("hid_relu", [P, TOK])
        hid = sb("hid", [P, TOK])
        lg = sb("lg", [P, CH, EXPERTS])
        top = sb("top", [P, CH, 8])
        o_sb = sb("o_sb", [P, CH, D])
        logits = sb("logits", [P, SEQS * CH, EXPERTS])
        gap = sb("gap", [P, SEQS * CH])
        first_w = sb("first_w", [P, 4, SEQS * CH])
        best = sb("best", [P, SEQS * CH])
        prob = sb("prob", [P, SEQS * CH, EXPERTS])
        any_p = sb("any_p", [P, P])
        flag_f = sb("flag_f", [1, 1])
        flag_i = sb("flag_i", [1, 1], I32)
        w1_sb = sb("w1_sb", [P, DC, EXPERTS, F])
        w2_sb = sb("w2_sb", [P, EXPERTS, D])

        s_bank = [bank(f"s_bank{i}") for i in range(2)]
        t_bank = [bank(f"t_bank{i}") for i in range(2)]
        o_bank = [bank(f"o_bank{i}") for i in range(2)]
        g_bank = [bank(f"g_bank{i}") for i in range(2)]

        weights_in = sem("weights_in")
        consts_made = sem("consts_made")
        ones_made = sem("ones_made")
        wo_masked = sem("wo_masked")
        ids_picked = sem("ids_picked")
        x_in = sem("x_in")
        xb_done = sem("xb_done")
        ln1_stats = sem("ln1_stats")
        ln1_chain = sem("ln1_chain")
        xn_done = sem("xn_done")
        xT_ready = sem("xT_ready")
        xT_done = sem("xT_done")
        q_ready, k_ready, v_ready = sem("q_ready"), sem("k_ready"), sem("v_ready")
        qk_done = sem("qk_done")
        part0_done = sem("part0_done")
        rest_done = sem("rest_done")
        part1_done = sem("part1_done")
        part2_done = sem("part2_done")
        parts_out = sem("parts_out")
        q_stacked, k_stacked = sem("q_stacked"), sem("k_stacked")
        v_done = sem("v_done")
        s_ready, max_done = sem("s_ready"), sem("max_done")
        max_turned = sem("max_turned")
        max_hi, max_lo = sem("max_hi"), sem("max_lo")
        max_in = [sem("max_in0"), sem("max_in1")]
        max_out = [sem("max_out0"), sem("max_out1")]
        t_ready, exp_done = sem("t_ready"), sem("exp_done")
        pv_ready = sem("pv_ready")
        oT_done = sem("oT_done")
        o_ready = sem("o_ready")
        inv_done = sem("inv_done")
        o_nat_done = sem("o_nat_done")
        o_turned_ready, o_turned_done = sem("o_turned_ready"), sem("o_turned_done")
        h1_ready, h1_done = sem("h1_ready"), sem("h1_done")
        ln2_stats = sem("ln2_stats")
        ln2_chain = sem("ln2_chain")
        z_done = sem("z_done")
        z_out = sem("z_out")
        zT_ready, zT_done = sem("zT_ready"), sem("zT_done")
        hid_ready, relu_done, hid_done = sem("hid_ready"), sem("relu_done"), sem("hid_done")
        lg_ready, lg_done = sem("lg_ready"), sem("lg_done")
        top_done = sem("top_done")
        gap_done = sem("gap_done")
        y_ready, y_done = sem("y_ready"), sem("y_done")
        out_out = sem("out_out")
        route_exp, route = sem("route_exp"), sem("route")
        flag_turned, flag_done = sem("flag_turned"), sem("flag_done")
        e_w_in, e_z_in, e_o_in = sem("e_w_in"), sem("e_z_in"), sem("e_o_in")
        e_zT_ready, e_zT_done = sem("e_zT_ready"), sem("e_zT_done")
        e_hid_ready, e_relu_done, e_hid_done = sem("e_hid_ready"), sem("e_relu_done"), sem("e_hid_done")
        e_y_ready, e_added, e_out = sem("e_y_ready"), sem("e_added"), sem("e_out")

        STEPS = SEQS + 3
        FIRST = 4
        LAST = FIRST + (SEQS - 2 - FIRST) // 3 * 3

        def stages(t):
            return tuple(0 <= t - lag < SEQS for lag in range(4))

        def steps(eng, step):
            for t in range(FIRST):
                step(t, t % 3, stages(t), True)
            with eng.Fori(FIRST, LAST - 2, 3) as t:
                for i in range(3):
                    step(t + i if i else t, (FIRST + i) % 3, (True,) * 4, False)
            for t in range(LAST, STEPS):
                step(t, t % 3, stages(t), True)

        held = (consts_made, CONSTS)

        def each_sequence(eng, body):
            body(0)
            with eng.Fori(1, SEQS) as s:
                body(s)

        block = ctx.enter_context(nc.Block())

        @block.sync
        def _(sp):
            loads = [
                (ids_sb[:, :], ids),
                (wq_sb[:, :, :], wq.rearrange("(c p) n -> p c n", p=P)),
                (wk_sb[:, :, :], wk.rearrange("(c p) n -> p c n", p=P)),
                (wv_sb[:, :, :], wv.rearrange("(c p) n -> p c n", p=P)),
                (wo_raw[:, :, :], wo.rearrange("(c p) n -> p c n", p=P)),
                (bqk[:, 0:DC], bq.rearrange("p c -> p c")),
                (bqk[:, DC:2 * DC], bk.rearrange("p c -> p c")),
                (bv_sb[:, :], bv.partition_broadcast(P)),
                (bo_sb[:, :], bo.partition_broadcast(P)),
                (mask_sb[:, :], mask),
                (ws1_sb[:, :, :], ws1.rearrange("(c p) n -> p c n", p=P)),
                (ws2_sb[:, :], ws2),
                (wr_sb[:, :, :], wr.rearrange("(c p) n -> p c n", p=P)),
            ]
            assert len(loads) == LOADS
            for dst, src in loads:
                sp.dma_start(dst, src).then_inc(weights_in, 16)

            def carry_max(s, half, turn):
                wait(sp, max_lo, 2 * s + half + 1)
                sp.dma_start(max_dram[half].rearrange("j (r q) -> r j q", q=P), max_parts[half][:, :, :]).then_inc(max_out[half], 16)
                wait(sp, max_out[half], 16 * (s + 1))
                sp.dma_start(stack_q[turn][ROWS:SROWS, 8 * half:8 * half + 8, :],
                             max_dram[half].rearrange("j (h n) -> j h n", n=TOK)).then_inc(max_in[half], 16)

            def step(t, turn, on, edge):
                a, b, c, d = on
                if c:
                    carry_max(t - 2, 1, (turn - 2) % 3)
                if a:
                    for which, (stack, stacked) in enumerate(((stack_q, q_stacked), (stack_k, k_stacked))):
                        waits_apart(sp, held, (stacked, 96 * t), (part2_done, 2 * t + which + 1))
                        sp.dma_start(parts_dram[which].rearrange("k (c p) n -> p k c n", p=P),
                                     parts[:, which, :, :, :]).then_inc(parts_out, 16)
                        if which == 0:
                            if b:
                                carry_max(t - 1, 0, (turn - 1) % 3)
                    for which, (stack, stacked) in enumerate(((stack_q, q_stacked), (stack_k, k_stacked))):
                        waits_apart(sp, held, (parts_out, 32 * t + 32), (t_ready, HEADS * (t - 2)))
                        for n, term in enumerate(TERMS):
                            src = parts_dram[which, term[which]].rearrange("(h d) n -> d h n", d=HD)
                            sp.dma_start(stack[turn][n * HD:(n + 1) * HD, :, :], src).then_inc(stacked, 16)
                elif b:
                    carry_max(t - 1, 0, (turn - 1) % 3)
                if d:
                    s = t - 3
                    wait(sp, z_done, CH * s + CH)
                    sp.dma_start(z_dram[bass.ds(s, 1), :, :].rearrange("o (c p) n -> p (o c) n", p=P), z[:, :, :]).then_inc(z_out, 16)
                    wait(sp, y_done, s + 1)
                    sp.dma_start(out[bass.ds(s, 1), :, :].rearrange("o (c p) n -> p (o c) n", p=P), o_sb[:, :, :]).then_inc(out_out, 16)

            steps(sp, step)
            sp.wait_ge(out_out, 16 * SEQS)
            sp.wait_ge(z_out, 16 * SEQS)

        @block.gpsimd
        def _(pool):
            pool.memset(ident[:, :], 0.0).then_inc(consts_made, 1)
            pool.wait_ge(consts_made, 1)
            pool.affine_select(out=ident[:, :], in_=ident[:, :], compare_op=ALU.not_equal, fill=1.0, base=0,
                               pattern=[[-1, P]], channel_multiplier=1).then_inc(consts_made, 1)
            pool.memset(minus_half[:, :], -0.5).then_inc(consts_made, 1)
            for u in range(2):
                pool.memset(neg_max[u][:, :], 0.0).then_inc(consts_made, 1)
            for i in range(3):
                pool.memset(v[:, i, :, :, HD:2 * HD], 1.0).then_inc(consts_made, 1)
            pool.memset(any_p[:, :], 0.0).then_inc(consts_made, 1)
            pool.wait_ge(consts_made, CONSTS)
            pool.wait_ge(weights_in, 16 * LOADS)

            def gather(s, turn):
                wait(pool, x_in, 16 * CH * s)
                pool.tensor_copy(ids_now[:, :], ids_sb[:, bass.ds(CH * s, CH)]).then_inc(ids_picked, 1)
                waits_apart(pool, held, (ids_picked, s + 1), (xb_done, s - 2), (xn_done, CH * (s - 2)))
                for c in range(CH):
                    pool.indirect_dma_start(out=x[:, turn, c, :], out_offset=None, in_=emb,
                                            in_offset=bass.IndirectOffsetOnAxis(ap=ids_now[:, c:c + 1], axis=0)
                                            ).then_inc(x_in, 16)

            def rsqrt(s, mv, rs, stats, chain, used):
                waits_apart(pool, held, (stats, 2 * CH * (s + 1)), (used, CH * s))
                ve, y, yy, f, r = (rs[:, i, :] for i in range(5))
                pool.tensor_scalar(ve, mv[:, :, 1], EPS, None, ALU.add).then_inc(chain, 1)
                wait(pool, chain, 6 * s + 1)
                pool.tensor_tensor(y, ve, minus_half[:, :], ALU.pow).then_inc(chain, 1)
                wait(pool, chain, 6 * s + 2)
                pool.tensor_tensor(yy, y, y, ALU.mult).then_inc(chain, 1)
                wait(pool, chain, 6 * s + 3)
                pool.tensor_tensor(f, yy, ve, ALU.mult).then_inc(chain, 1)
                waits_apart(pool, held, (chain, 6 * s + 4))
                pool.tensor_scalar(yy, f, -0.5, 1.5, ALU.mult, ALU.add).then_inc(chain, 1)
                wait(pool, chain, 6 * s + 5)
                pool.tensor_tensor(r, y, yy, ALU.mult).then_inc(chain, 1)

            def step(t, turn, on, edge):
                a, b, c, d = on
                if a:
                    for which in range(2):
                        wait(pool, part0_done, 2 * t + which + 1)
                        wait(pool, part1_done, 2 * t + which - 1)
                        wait(pool, part2_done, 2 * t + which - 1)
                        pool.tensor_tensor(qk_rest[:, which, :, :], qk[:, which, :, :], parts[:, which, 0, :, :],
                                           ALU.subtract).then_inc(rest_done, 1)
                    for which in range(2):
                        wait(pool, part1_done, 2 * t + which + 1)
                        wait(pool, parts_out, 32 * t)
                        wait(pool, rest_done, 2 * t + which + 1)
                        pool.tensor_tensor(parts[:, which, 2, :, :], qk_rest[:, which, :, :], parts[:, which, 1, :, :],
                                           ALU.subtract).then_inc(part2_done, 1)
                if d:
                    rsqrt(t - 3, mv2, rs2, ln2_stats, ln2_chain, z_done)
                if a:
                    wait(pool, h1_done, t - 2)
                    wait(pool, x_in, 16 * CH * (t + 1))
                    for ch in range(CH):
                        ins = pool.tensor_tensor(xb[:, turn, ch, :], x[:, turn, ch, :], bo_sb[:, :], ALU.add)
                    ins.then_inc(xb_done, 1)
                if d:
                    wait(pool, relu_done, t - 2)
                    wait(pool, y_ready, t - 3)
                    pool.tensor_tensor(hid[:, :], hid_relu[:, :], hid_relu[:, :], ALU.mult).then_inc(hid_done, 1)
                if not edge or t + 1 < SEQS:
                    rsqrt(t + 1, mv1, rs1, ln1_stats, ln1_chain, xn_done)
                if not edge or t + 2 < SEQS:
                    gather(t + 2, (turn + 2) % 3)

            gather(0, 0)
            rsqrt(0, mv1, rs1, ln1_stats, ln1_chain, xn_done)
            gather(1, 1)
            steps(pool, step)

        @block.scalar
        def _(act):
            act.wait_ge(weights_in, 16 * LOADS)
            act.wait_ge(consts_made, CONSTS)

            def first_max_part(s, half):
                wait(act, max_turned, 2 * s + half + 1)
                wait(act, max_out[half], 16 * s)
                act.activation(max_parts[half][:, 0, :], g_bank[half ^ 1][0:HEADS, 0:P], ACT.Copy).then_inc(max_hi, 1)

            def take_output(s, pair):
                wait(act, pv_ready, 4 * s + 2 * pair + 2)
                wait(act, o_ready, CH * s)
                act.activation(oT[:, 2 * pair:2 * pair + 2, :], o_bank[pair][:, :].rearrange("p (g n) -> p g n", g=2),
                               ACT.Copy).then_inc(oT_done, 1)

            def take_qk(s, which, bank):
                wait(act, (q_ready, k_ready)[which], s + 1)
                wait(act, part0_done, 2 * s + which - 1)
                wait(act, rest_done, 2 * s + which - 1)
                for ch in range(DC):
                    act.activation(qk[:, which, ch, :], bank[:, ch * TOK:(ch + 1) * TOK], ACT.Identity,
                                   bias=bqk[:, which * DC + ch:which * DC + ch + 1]).then_inc(qk_done, 1)

            def step(t, turn, on, edge):
                a, b, c, d = on
                for h in range(HEADS):
                    if c:
                        n = HEADS * (t - 2) + h
                        wait(act, t_ready, n + 1)
                        wait(act, pv_ready, 4 * (t - 2) + (h - 8) // GH + 1)
                        act.activation(probs[:, h % 8, :, :], t_bank[h % 2][:, :].rearrange("p (c n) -> p c n", c=CH),
                                       ACT.Exp, scale=HD ** -0.5).then_inc(exp_done, 1)
                    if h == 0 and c:
                        first_max_part(t - 2, 1)
                    if h == 1 and a:
                        wait(act, xT_ready, t + 1)
                        wait(act, v_ready, t)
                        act.activation(xT[:, :, :], g_bank[1][:, :].rearrange("p (c n) -> p c n", c=DC), ACT.Copy).then_inc(xT_done, 1)
                    if h == 2 and d:
                        take_output(t - 3, 1)
                    if h == 3 and a:
                        take_qk(t, 0, g_bank[0])
                    if h == 6 and a:
                        take_qk(t, 1, g_bank[1])
                    if h == 7 and d:
                        wait(act, o_turned_ready, t - 2)
                        wait(act, h1_ready, t - 3)
                        act.activation(o_turned[:, :, :], g_bank[0][:, :].rearrange("p (c n) -> p c n", c=DC), ACT.Copy).then_inc(o_turned_done, 1)
                    if h == 10 and b:
                        first_max_part(t - 1, 0)
                    if h == 11 and c:
                        take_output(t - 2, 0)
                    if h == 13 and d:
                        wait(act, zT_ready, t - 2)
                        wait(act, lg_ready, t - 3)
                        act.activation(zT[:, :, :], g_bank[0][:, :].rearrange("p (c n) -> p c n", c=DC), ACT.Copy).then_inc(zT_done, 1)
                    if h == 14 and d:
                        wait(act, hid_ready, t - 2)
                        wait(act, hid_done, t - 3)
                        act.activation(hid_relu[:, :], g_bank[1][:, 0:TOK], ACT.Relu).then_inc(relu_done, 1)
                    if h == 15 and d:
                        wait(act, lg_ready, t - 2)
                        wait(act, gap_done, 2 * (t - 3))
                        act.activation(lg[:, :, :], g_bank[0][:, 0:CH * EXPERTS].rearrange("p (c e) -> p c e", c=CH),
                                       ACT.Copy).then_inc(lg_done, 1)

            steps(act, step)
            act.wait_ge(gap_done, 2 * SEQS)
            act.activation(first_w[:, 0, :], gap[:, :], ACT.Exp).then_inc(route_exp, 1)

            act.wait_ge(flag_done, 1)
            flag = act.value_load(flag_i[0:1, 0:1], min_val=0, max_val=1)
            with act.If(flag > 0):
                def route_one(s):
                    act.wait_ge(e_zT_ready, s + 1)
                    act.activation(zT[:, :, :], g_bank[0][:, :].rearrange("p (c n) -> p c n", c=DC), ACT.Copy).then_inc(e_zT_done, 1)
                    for e in range(EXPERTS):
                        act.wait_ge(e_hid_ready, s * EXPERTS + (e + 1))
                        act.activation(hid_relu[:, :], g_bank[1][:, 0:TOK], ACT.Relu).then_inc(e_relu_done, 1)
                        act.wait_ge(e_relu_done, s * EXPERTS + (e + 1))
                        act.activation(hid[:, :], hid_relu[:, :], ACT.Square).then_inc(e_hid_done, 1)

                each_sequence(act, route_one)

        @block.vector
        def _(dve):
            for i in range(3):
                dve.memset(stack_k[i][ROWS:SROWS, :, :], 1.0).then_inc(ones_made, 1)
            dve.wait_ge(weights_in, 16 * LOADS)
            dve.wait_ge(consts_made, CONSTS)
            for ch in range(DC):
                dve.tensor_scalar(wo_sb[:, ch, :], wo_raw[:, ch, :], mask_sb[:, ch:ch + 1], None, ALU.mult).then_inc(wo_masked, 1)

            def statistics(src, s, stat, mv, stats, chain, before=None):
                wait(dve, chain, 6 * s)
                for ch in range(CH):
                    dve.bn_stats(stat[:, ch, :], src[:, ch, :]).then_inc(stats, 1)
                for ch in range(CH):
                    waits_apart(dve, held, (stats, 2 * CH * s + ch + 1))
                    dve.bn_aggr(mv[:, ch, :], stat[:, ch, :]).then_inc(stats, 1)

            def norm(dst, src, s, mv, rs, stats, chain, done):
                wait(dve, chain, 6 * (s + 1))
                wait(dve, stats, 2 * CH * (s + 1))
                for ch in range(CH):
                    dve.tensor_scalar(dst[:, ch, :], src[:, ch, :], mv[:, ch, 0:1], rs[:, 4, ch:ch + 1],
                                      ALU.subtract, ALU.mult).then_inc(done, 1)

            def norm_x_1(s, turn):
                wait(dve, x_in, 16 * CH * (s + 1))
                statistics(x[:, turn, :, :], s, stat1, mv1, ln1_stats, ln1_chain)

            def norm_x_2(s, turn):
                wait(dve, xT_ready, s)
                norm(xn, x[:, turn, :, :], s, mv1, rs1, ln1_stats, ln1_chain, xn_done)

            def second_max_part(s, half):
                wait(dve, max_hi, 2 * s + half + 1)
                dve.tensor_tensor(max_parts[half][:, 1, :], g_bank[half ^ 1][0:HEADS, 0:P], max_parts[half][:, 0, :],
                                  ALU.subtract).then_inc(max_lo, 1)

            def divide(s, ch):
                wait(dve, o_ready, CH * s + ch + 1)
                wait(dve, o_turned_ready, s)
                o = g_bank[ch ^ 1][:, :].rearrange("p (h e) -> p h e", e=2 * HD)
                dve.reciprocal(inv_sum[:, ch, :], o[:, :, HD]).then_inc(inv_done, 1)
                wait(dve, inv_done, CH * s + ch + 1)
                dve.tensor_tensor(o_nat[:, ch, :, :], o[:, :, 0:HD],
                                  inv_sum[:, ch, :].unsqueeze(2).broadcast_to([P, HEADS, HD]), ALU.mult).then_inc(o_nat_done, 1)

            def step(t, turn, on, edge):
                a, b, c, d = on
                for h in range(HEADS):
                    if b:
                        n = HEADS * (t - 1) + h
                        half = h // 8
                        wait(dve, s_ready, n + 1)
                        wait(dve, max_turned, 2 * (t - 1) + half - 1)
                        at = (h % 8) * CH
                        dve.tensor_reduce(neg_max[half][:, at:at + CH], s_bank[h % 2][:, :].rearrange("p (c n) -> p c n", c=CH),
                                          AX.X, ALU.max, negate=True).then_inc(max_done, 1)
                    if h == 0 and c:
                        second_max_part(t - 2, 1)
                    if h == 3 and d:
                        divide(t - 3, 0)
                    if h == 4 and d:
                        divide(t - 3, 1)
                    for which in range(2):
                        if h == (5, 7)[which] and a:
                            wait(dve, qk_done, 2 * DC * t + DC * (which + 1))
                            wait(dve, parts_out, 32 * t)
                            dve.tensor_copy(parts[:, which, 0, :, :], qk[:, which, :, :]).then_inc(part0_done, 1)
                        if h == (8, 10)[which] and a:
                            wait(dve, rest_done, 2 * t + which + 1)
                            dve.tensor_copy(parts[:, which, 1, :, :], qk_rest[:, which, :, :]).then_inc(part1_done, 1)
                    if h == 8 and a:
                        wait(dve, v_ready, t + 1)
                        wait(dve, pv_ready, 4 * (t - 2))
                        for ch in range(CH):
                            ins = dve.tensor_tensor(v[:, turn, ch, :, 0:HD],
                                                    g_bank[1][:, ch * D:(ch + 1) * D].rearrange("p (h e) -> p h e", e=HD),
                                                    bv_sb[:, :].rearrange("p (h e) -> p h e", e=HD), ALU.add)
                        ins.then_inc(v_done, 1)
                    if h == 9 and d:
                        wait(dve, h1_ready, t - 2)
                        wait(dve, xb_done, t - 2)
                        wait(dve, y_done, t - 3)
                        dve.tensor_tensor(h1[:, :, :], g_bank[0][:, :].rearrange("p (c n) -> p c n", c=CH),
                                          xb[:, turn, :, :], ALU.add).then_inc(h1_done, 1)
                        wait(dve, h1_done, t - 2)
                        statistics(h1, t - 3, stat2, mv2, ln2_stats, ln2_chain)
                    if h == 10 and b:
                        second_max_part(t - 1, 0)
                    if h == 12 and d:
                        wait(dve, zT_ready, t - 3)
                        wait(dve, z_out, 16 * (t - 3))
                        norm(z, h1, t - 3, mv2, rs2, ln2_stats, ln2_chain, z_done)
                    if h == 13 and (not edge or t + 1 < SEQS):
                        norm_x_1(t + 1, (turn + 1) % 3)
                if not edge or t + 1 < SEQS:
                    norm_x_2(t + 1, (turn + 1) % 3)
                if d:
                    s = t - 3
                    waits_apart(dve, held, (lg_done, s + 1), (gap_done, 2 * s))
                    for ch in range(CH):
                        dve.max(top[:, ch, :], lg[:, ch, :]).then_inc(top_done, 1)
                    dve.tensor_copy(logits[:, bass.ds(CH * s, CH), :], lg[:, :, :]).then_inc(gap_done, 1)
                    wait(dve, top_done, CH * s + CH)
                    dve.tensor_tensor(gap[:, bass.ds(CH * s, CH)], top[:, :, 1], top[:, :, 0], ALU.subtract).then_inc(gap_done, 1)
                    wait(dve, y_ready, s + 1)
                    wait(dve, out_out, 16 * s)
                    dve.tensor_tensor(o_sb[:, :, :], g_bank[1][:, :].rearrange("p (c n) -> p c n", c=CH), h1[:, :, :],
                                      ALU.add).then_inc(y_done, 1)

            norm_x_1(0, 0)
            norm_x_2(0, 0)
            steps(dve, step)

            n = [0]

            def link(ins):
                n[0] += 1
                ins.then_inc(route, 1)
                dve.wait_ge(route, n[0])

            dve.wait_ge(route_exp, 1)
            link(dve.tensor_scalar(first_w[:, 1, :], first_w[:, 0, :], 1.0, None, ALU.add))
            link(dve.reciprocal(first_w[:, 2, :], first_w[:, 1, :]))
            link(dve.tensor_scalar(first_w[:, 3, :], first_w[:, 2, :], 1.0, None, ALU.is_ge))
            link(dve.tensor_reduce(any_p[:, 0:1], first_w[:, 3, :], AX.X, ALU.max))
            dve.wait_ge(flag_turned, 1)
            link(dve.tensor_reduce(flag_f[:, :], g_bank[0][0:1, 0:P], AX.X, ALU.max))
            dve.tensor_copy(flag_i[:, :], flag_f[:, :]).then_inc(flag_done, 1)

            dve.wait_ge(flag_done, 1)
            flag = dve.value_load(flag_i[0:1, 0:1], min_val=0, max_val=1)
            with dve.If(flag > 0):
                link(dve.tensor_reduce(best[:, :], logits[:, :, :], AX.X, ALU.max))
                link(dve.tensor_tensor(prob[:, :, :], logits[:, :, :],
                                       best[:, :].unsqueeze(2).broadcast_to([P, SEQS * CH, EXPERTS]), ALU.is_ge))
                link(dve.tensor_tensor(prob[:, :, :], prob[:, :, :],
                                       first_w[:, 3, :].unsqueeze(2).broadcast_to([P, SEQS * CH, EXPERTS]), ALU.mult))
                def route_one(s):
                    dve.wait_ge(e_o_in, s * 16 + 16)
                    for e in range(EXPERTS):
                        dve.wait_ge(e_y_ready, s * EXPERTS + (e + 1))
                        for ch in range(CH):
                            k = (s * EXPERTS + e) * CH + ch
                            if e:
                                dve.wait_ge(e_added, k - CH + 1)
                            dve.tensor_copy(top[:, ch, 0:1], prob[:, bass.ds(s * CH + ch, 1), e]).then_inc(route, 1)
                            dve.wait_ge(route, k + (ROUTE + 1))
                            dve.scalar_tensor_tensor(out=o_sb[:, ch, :], in0=g_bank[0][:, ch * D:(ch + 1) * D],
                                                     scalar=top[:, ch, 0:1], in1=o_sb[:, ch, :],
                                                     op0=ALU.mult, op1=ALU.add).then_inc(e_added, 1)

                each_sequence(dve, route_one)
            assert n[0] == ROUTE

        @block.tensor
        def _(pe):
            pe.wait_ge(weights_in, 16 * LOADS)
            pe.wait_ge(consts_made, CONSTS)
            pe.wait_ge(wo_masked, DC)
            pe.wait_ge(ones_made, 3)

            def turn_tile(bank, src, last_sem):
                for dc in range(DC):
                    for ch in range(CH):
                        at = dc * TOK + ch * P
                        ins = pe.transpose(bank[:, at:at + P], src[:, ch, dc * P:(dc + 1) * P], ident[:, :])
                ins.then_inc(last_sem, 1)

            def project_turned(bank, w, ready):
                for m in range(DC):
                    for dc in range(DC):
                        ins = pe.matmul(bank[:, m * TOK:(m + 1) * TOK], w[:, dc, m * P:(m + 1) * P], xT[:, dc, :],
                                        start=(dc == 0), stop=(dc == DC - 1))
                ins.then_inc(ready, 1)

            def project(bank, src, w, ready):
                for ch in range(CH):
                    for dc in range(DC):
                        ins = pe.matmul(bank[:, ch * D:(ch + 1) * D], src[:, dc, ch * P:(ch + 1) * P], w[:, dc, :],
                                        start=(dc == 0), stop=(dc == DC - 1))
                ins.then_inc(ready, 1)

            def scores(s, h, turn):
                if h == 0:
                    wait(pe, q_stacked, 96 * (s + 1))
                    wait(pe, k_stacked, 96 * (s + 1))
                wait(pe, max_done, HEADS * s + h - 1)
                for ch in range(CH):
                    ins = pe.matmul(s_bank[h % 2][:, ch * TOK:(ch + 1) * TOK],
                                    stack_q[turn][0:ROWS, h, ch * P:(ch + 1) * P], stack_k[turn][0:ROWS, h, :],
                                    start=True, stop=True)
                ins.then_inc(s_ready, 1)

            def scores_turned(s, h, turn):
                if h % 8 == 0:
                    wait(pe, max_in[h // 8], 16 * (s + 1))
                wait(pe, exp_done, HEADS * s + h - 1)
                for ch in range(CH):
                    ins = pe.matmul(t_bank[h % 2][:, ch * TOK:(ch + 1) * TOK],
                                    stack_k[turn][0:SROWS, h, ch * P:(ch + 1) * P], stack_q[turn][0:SROWS, h, :],
                                    start=True, stop=True)
                ins.then_inc(t_ready, 1)

            def attend(s, g, turn):
                wait(pe, exp_done, HEADS * s + GH * (g + 1))
                wait(pe, oT_done, 2 * s + g // 2 - 1)
                if g == 0:
                    wait(pe, v_done, s + 1)
                at = (g % 2) * TOK
                for ch in range(CH):
                    for i in range(GH):
                        h = GH * g + i
                        ins = pe.matmul(o_bank[g // 2][32 * i:32 * i + 32, at:at + TOK], v[:, turn, ch, h, :],
                                        probs[:, h % 8, ch, :], start=(ch == 0), stop=(ch == CH - 1),
                                        skip_group_check=True)
                ins.then_inc(pv_ready, 1)

            def turn_max(s, half):
                wait(pe, max_done, HEADS * s + 8 * (half + 1))
                pe.transpose(g_bank[half ^ 1][:, 0:P], neg_max[half][:, :], ident[:, :]).then_inc(max_turned, 1)

            def step(t, turn, on, edge):
                a, b, c, d = on
                if edge:
                    wait(pe, v_done, min(t, SEQS))
                    wait(pe, qk_done, 2 * DC * min(t, SEQS))
                    wait(pe, max_lo, 2 * (t - 2) + 1 if t - 1 <= SEQS else 2 * SEQS)
                    wait(pe, y_done, t - 3)
                    wait(pe, lg_done, t - 3)
                for h in range(HEADS):
                    if b:
                        scores(t - 1, h, (turn - 1) % 3)
                    if h == 0 and c:
                        wait(pe, lg_done, t - 3)
                        turn_max(t - 2, 1)
                    if h == 8 and c:
                        pass
                    if c:
                        scores_turned(t - 2, h, (turn - 2) % 3)
                        if h % GH == 1 and h > GH:
                            attend(t - 2, h // GH - 1, (turn - 2) % 3)
                    if h == 1 and d:
                        attend(t - 3, 3, turn)
                    if h == 1 and a:
                        wait(pe, y_done, t - 3)
                        wait(pe, xn_done, CH * (t + 1))
                        turn_tile(g_bank[1], xn, xT_ready)
                    if h == 2 and a:
                        wait(pe, max_lo, 2 * (t - 2) + 2)
                        wait(pe, xT_done, t + 1)
                        project_turned(g_bank[0], wq_sb, q_ready)
                    if h in (3, 4) and d:
                        ch = h - 3
                        wait(pe, oT_done, 2 * (t - 3) + 2)
                        if ch == 0 and a:
                            wait(pe, xT_done, t + 1)
                        if ch == 1 and a:
                            wait(pe, qk_done, 2 * DC * t + DC)
                        if ch == 1 and c and not a:
                            wait(pe, max_lo, 2 * (t - 2) + 2)
                        for g in range(HEADS // GH):
                            ins = pe.transpose(g_bank[ch ^ 1][:, g * P:(g + 1) * P], oT[:, g, ch * P:(ch + 1) * P], ident[:, :])
                        ins.then_inc(o_ready, 1)
                    if h == 5 and a:
                        wait(pe, o_nat_done, CH * (t - 3) + 1)
                        project_turned(g_bank[1], wk_sb, k_ready)
                    if h == 6 and d:
                        wait(pe, o_nat_done, CH * (t - 3) + 2)
                        turn_tile(g_bank[0], o_nat[:, :, :, :].rearrange("p c h e -> p c (h e)"), o_turned_ready)
                    if h == 7 and a:
                        wait(pe, qk_done, 2 * DC * (t + 1))
                        project(g_bank[1], xT, wv_sb, v_ready)
                    if h == 8 and d:
                        wait(pe, o_turned_done, t - 2)
                        project(g_bank[0], o_turned, wo_sb, h1_ready)
                    if h == 9 and b:
                        if a:
                            wait(pe, v_done, t + 1)
                        turn_max(t - 1, 0)
                    if h == 13 and d:
                        wait(pe, z_done, CH * (t - 2))
                        turn_tile(g_bank[0], z, zT_ready)
                    if h == 14 and d:
                        wait(pe, zT_done, t - 2)
                        if b:
                            wait(pe, max_lo, 2 * (t - 1) + 1)
                        for dc in range(DC):
                            ins = pe.matmul(g_bank[1][:, 0:TOK], ws1_sb[:, dc, :], zT[:, dc, :],
                                            start=(dc == 0), stop=(dc == DC - 1))
                        ins.then_inc(hid_ready, 1)
                        for ch in range(CH):
                            for dc in range(DC):
                                ins = pe.matmul(g_bank[0][:, ch * EXPERTS:(ch + 1) * EXPERTS], zT[:, dc, ch * P:(ch + 1) * P],
                                                wr_sb[:, dc, :], start=(dc == 0), stop=(dc == DC - 1))
                        ins.then_inc(lg_ready, 1)
                if d:
                    wait(pe, hid_done, t - 2)
                    for ch in range(CH):
                        ins = pe.matmul(g_bank[1][:, ch * D:(ch + 1) * D], hid[:, ch * P:(ch + 1) * P], ws2_sb[:, :],
                                        start=True, stop=True)
                    ins.then_inc(y_ready, 1)

            steps(pe, step)
            pe.wait_ge(lg_done, SEQS)
            pe.wait_ge(route, 4)
            pe.transpose(g_bank[0][:, 0:P], any_p[:, :], ident[:, :]).then_inc(flag_turned, 1)

            pe.wait_ge(flag_done, 1)
            flag = pe.value_load(flag_i[0:1, 0:1], min_val=0, max_val=1)
            with pe.If(flag > 0):
                pe.wait_ge(e_w_in, 16 * (DC + 1))
                def route_one(s):
                    pe.wait_ge(e_z_in, s * 16 + 16)
                    wait(pe, e_added, s * (EXPERTS * CH))
                    turn_tile(g_bank[0], z, e_zT_ready)
                    pe.wait_ge(e_zT_done, s + 1)
                    for e in range(EXPERTS):
                        wait(pe, e_relu_done, s * EXPERTS + e)
                        for dc in range(DC):
                            ins = pe.matmul(g_bank[1][:, 0:TOK], w1_sb[:, dc, e, :], zT[:, dc, :],
                                            start=(dc == 0), stop=(dc == DC - 1))
                        ins.then_inc(e_hid_ready, 1)
                        pe.wait_ge(e_hid_done, s * EXPERTS + (e + 1))
                        wait(pe, e_added, (s * EXPERTS + e) * CH)
                        for ch in range(CH):
                            ins = pe.matmul(g_bank[0][:, ch * D:(ch + 1) * D], hid[:, ch * P:(ch + 1) * P], w2_sb[:, e, :],
                                            start=True, stop=True)
                        ins.then_inc(e_y_ready, 1)

                each_sequence(pe, route_one)

        @block.sync
        def _(sp):
            sp.wait_ge(flag_done, 1)
            flag = sp.value_load(flag_i[0:1, 0:1], min_val=0, max_val=1)
            with sp.If(flag > 0):
                for ch in range(DC):
                    sp.dma_start(w1_sb[:, ch, :, :], w1[:, ch * P:(ch + 1) * P, :].rearrange("e p f -> p e f")).then_inc(e_w_in, 16)
                sp.dma_start(w2_sb[:, :, :], w2.rearrange("e f n -> f e n")).then_inc(e_w_in, 16)
                def route_one(s):
                    wait(sp, e_zT_ready, s)
                    sp.dma_start(z[:, :, :], z_dram[bass.ds(s, 1), :, :].rearrange("o (c p) n -> p (o c) n", p=P)).then_inc(e_z_in, 16)
                    wait(sp, e_out, s * 16)
                    sp.dma_start(o_sb[:, :, :], out[bass.ds(s, 1), :, :].rearrange("o (c p) n -> p (o c) n", p=P)).then_inc(e_o_in, 16)
                    sp.wait_ge(e_added, (s + 1) * (EXPERTS * CH))
                    sp.dma_start(out[bass.ds(s, 1), :, :].rearrange("o (c p) n -> p (o c) n", p=P), o_sb[:, :, :]).then_inc(e_out, 16)

                each_sequence(sp, route_one)
                sp.wait_ge(e_out, SEQS * 16)


LOADS = 13
CONSTS = 9
ROUTE = 8


_ORDER = ["ids", "emb", "wq", "bq", "wk", "bk", "wv", "bv", "wo", "bo", "mask", "ws1", "ws2", "w1", "w2", "wr"]


def kernel(x, L0_tok_embeddings, L0_attn_Wq, L0_attn_bq, L0_attn_Wk, L0_attn_bk, L0_attn_Wv, L0_attn_bv,
           L0_attn_Wo, L0_attn_bo, L0_attn_head_mask, L0_ffn_Ws1, L0_ffn_Ws2, L0_ffn_W1, L0_ffn_W2, L0_ffn_Wr):
    import numpy as np
    import concourse.bacc as bacc
    from concourse import mybir as mb
    from concourse.bass_utils import run_bass_kernel_spmd

    seqs, tok = x.shape
    d = L0_tok_embeddings.shape[1]
    heads = L0_attn_head_mask.shape[0]
    c = np.ascontiguousarray
    data = {
        "ids": c(np.asarray(x).reshape(-1, 128).T),
        "emb": c(np.asarray(L0_tok_embeddings)),
        "wq": c(np.asarray(L0_attn_Wq).T), "wk": c(np.asarray(L0_attn_Wk).T),
        "wv": c(np.asarray(L0_attn_Wv).T), "wo": c(np.asarray(L0_attn_Wo).T),
        "bq": c(np.asarray(L0_attn_bq).reshape(-1, 128).T), "bk": c(np.asarray(L0_attn_bk).reshape(-1, 128).T),
        "bv": c(np.asarray(L0_attn_bv)), "bo": c(np.asarray(L0_attn_bo)),
        "mask": c(np.repeat(np.asarray(L0_attn_head_mask), d // heads).reshape(-1, 128).T),
        "ws1": c(np.asarray(L0_ffn_Ws1)), "ws2": c(np.asarray(L0_ffn_Ws2)),
        "w1": c(np.asarray(L0_ffn_W1)), "w2": c(np.asarray(L0_ffn_W2)), "wr": c(np.asarray(L0_ffn_Wr)),
    }
    nc = bacc.Bacc("TRN2", target_bir_lowering=False, num_devices=1)
    arrays, args = {}, []
    for name in _ORDER:
        arrays[f"in_{name}"] = data[name]
        args.append(nc.dram_tensor(f"in_{name}", data[name].shape, mb.dt.from_np(data[name].dtype), kind="ExternalInput").ap())
    out = nc.dram_tensor("out_0", (seqs, tok, d), mb.dt.float32, kind="ExternalOutput").ap()
    tower(nc, *args, out)
    r = run_bass_kernel_spmd(nc, [arrays], core_ids=[0])
    return r.results[0]["out_0"]
```

```python
import concourse.bass as bass
from concourse import mybir
from contextlib import ExitStack

F32 = mybir.dt.float32
BF16 = mybir.dt.bfloat16
I32 = mybir.dt.int32
ALU = mybir.AluOpType
ACT = mybir.ActivationFunctionType
AX = mybir.AxisListType

P = 128
TERMS = [(0, 0), (0, 1), (0, 2), (1, 0), (1, 1), (2, 0)]
EPS = 1e-5


def wait(eng, sem, value):
    if not isinstance(value, int) or value > 0:
        eng.wait_ge(sem, value)


def waits_apart(eng, held, *waits):
    if all(isinstance(value, int) for _, value in waits):
        for sem, value in waits:
            wait(eng, sem, value)
    else:
        waits = [(sem, eng.to_reg(value)) for sem, value in waits]
        eng.wait_ge(*held)
        for sem, value in waits:
            eng.wait_ge(sem, value)


def tower(nc, ids, emb, wq, bq, wk, bk, wv, bv, wo, bo, mask, ws1, ws2, w1, w2, wr, out):
    SEQS, TOK, D = out.shape
    HEADS = 16
    HD = D // HEADS
    CH = TOK // P
    DC = D // P
    HC = P // HD
    GH = 4
    F = ws1.shape[1]
    EXPERTS = wr.shape[1]
    ROWS = len(TERMS) * HD
    SROWS = ROWS + 2
    W = DC * TOK

    ctx = ExitStack()
    with ctx:
        def sb(name, shape, dt=F32):
            return ctx.enter_context(nc.sbuf_tensor(name, shape, dt))

        def bank(name):
            return ctx.enter_context(nc.psum_tensor(name, [P, W], F32))

        def sem(name):
            return ctx.enter_context(nc.semaphore(name))

        parts_dram = nc.dram_tensor("parts_dram", [2, 3, D, TOK], BF16, kind="Internal").ap()
        max_dram = nc.dram_tensor("max_dram", [2, 2, HEADS // 2 * TOK], BF16, kind="Internal").ap()
        z_dram = nc.dram_tensor("z_dram", [SEQS, TOK, D], F32, kind="Internal").ap()

        ident = sb("ident", [P, P])
        ids_sb = sb("ids_sb", [P, SEQS * CH], I32)
        ids_now = sb("ids_now", [P, CH], I32)
        wq_sb, wk_sb, wv_sb, wo_sb, wo_raw = (sb(n, [P, DC, D]) for n in ("wq_sb", "wk_sb", "wv_sb", "wo_sb", "wo_raw"))
        bqk = sb("bqk", [P, 2 * DC])
        bv_sb = sb("bv_sb", [P, D])
        bo_sb = sb("bo_sb", [P, D])
        mask_sb = sb("mask_sb", [P, DC])
        ws1_sb = sb("ws1_sb", [P, DC, F])
        ws2_sb = sb("ws2_sb", [P, D])
        wr_sb = sb("wr_sb", [P, DC, EXPERTS])
        minus_half = sb("minus_half", [P, CH])

        x = sb("x", [P, 3, CH, D])
        stat1, mv1 = sb("stat1", [P, CH, 6]), sb("mv1", [P, CH, 2])
        rs1 = sb("rs1", [P, 5, CH])
        xn = sb("xn", [P, CH, D])
        xT = sb("xT", [P, DC, TOK])
        qk = sb("qk", [P, 2, DC, TOK])
        qk_rest = sb("qk_rest", [P, 2, DC, TOK])
        parts = sb("parts", [P, 2, 3, DC, TOK], BF16)
        stack_q = [sb(f"stack_q{i}", [P, HEADS, TOK], BF16) for i in range(3)]
        stack_k = [sb(f"stack_k{i}", [P, HEADS, TOK], BF16) for i in range(3)]
        stacks = (stack_q, stack_k)
        v = sb("v", [P, 3, CH, HEADS, 2 * HD])
        neg_max = [sb(f"neg_max{u}", [P, P]) for u in range(2)]
        max_parts = [sb(f"max_parts{u}", [HEADS, 2, P], BF16) for u in range(2)]
        probs = sb("probs", [P, 8, CH, TOK])
        oT = sb("oT", [P, HEADS // GH, TOK])
        inv_sum = sb("inv_sum", [P, CH, HEADS])
        o_nat = sb("o_nat", [P, CH, HEADS, HD])
        o_turned = sb("o_turned", [P, DC, TOK])
        xb = sb("xb", [P, 3, CH, D])
        h1 = sb("h1", [P, CH, D])
        stat2, mv2 = sb("stat2", [P, CH, 6]), sb("mv2", [P, CH, 2])
        rs2 = sb("rs2", [P, 5, CH])
        z = sb("z", [P, CH, D])
        zT = sb("zT", [P, DC, TOK])
        hid_relu = sb("hid_relu", [P, TOK])
        hid = sb("hid", [P, TOK])
        lg = sb("lg", [P, CH, EXPERTS])
        top = sb("top", [P, CH, 8])
        o_sb = sb("o_sb", [P, CH, D])
        logits = sb("logits", [P, SEQS * CH, EXPERTS])
        gap = sb("gap", [P, SEQS * CH])
        first_w = sb("first_w", [P, 4, SEQS * CH])
        best = sb("best", [P, SEQS * CH])
        prob = sb("prob", [P, SEQS * CH, EXPERTS])
        any_p = sb("any_p", [P, P])
        flag_f = sb("flag_f", [1, 1])
        flag_i = sb("flag_i", [1, 1], I32)
        w1_sb = sb("w1_sb", [P, DC, EXPERTS, F])
        w2_sb = sb("w2_sb", [P, EXPERTS, D])

        s_bank = [bank(f"s_bank{i}") for i in range(2)]
        t_bank = [bank(f"t_bank{i}") for i in range(2)]
        o_bank = [bank(f"o_bank{i}") for i in range(2)]
        g_bank = [bank(f"g_bank{i}") for i in range(2)]

        weights_in = sem("weights_in")
        consts_made = sem("consts_made")
        ones_made = sem("ones_made")
        wo_masked = sem("wo_masked")
        ids_picked = sem("ids_picked")
        x_in = sem("x_in")
        xb_done = sem("xb_done")
        ln1_stats = sem("ln1_stats")
        ln1_chain = sem("ln1_chain")
        xn_done = sem("xn_done")
        xT_ready = sem("xT_ready")
        xT_done = sem("xT_done")
        q_ready, k_ready, v_ready = sem("q_ready"), sem("k_ready"), sem("v_ready")
        qk_done = sem("qk_done")
        part0_done = sem("part0_done")
        rest_done = sem("rest_done")
        part1_done = sem("part1_done")
        part2_done = sem("part2_done")
        parts_out = [sem("q_parts_out"), sem("k_parts_out")]
        stacked = [sem("q_stacked"), sem("k_stacked")]
        v_done = sem("v_done")
        s_ready, max_done = sem("s_ready"), sem("max_done")
        max_turned = sem("max_turned")
        max_hi, max_lo = sem("max_hi"), sem("max_lo")
        max_in = [sem("max_in0"), sem("max_in1")]
        max_out = [sem("max_out0"), sem("max_out1")]
        t_ready, exp_done = sem("t_ready"), sem("exp_done")
        pv_ready = sem("pv_ready")
        oT_done = sem("oT_done")
        o_ready = sem("o_ready")
        inv_done = sem("inv_done")
        o_nat_done = sem("o_nat_done")
        o_turned_ready, o_turned_done = sem("o_turned_ready"), sem("o_turned_done")
        h1_ready, h1_done = sem("h1_ready"), sem("h1_done")
        ln2_stats = sem("ln2_stats")
        ln2_chain = sem("ln2_chain")
        z_done = sem("z_done")
        z_out = sem("z_out")
        zT_ready, zT_done = sem("zT_ready"), sem("zT_done")
        hid_ready, relu_done, hid_done = sem("hid_ready"), sem("relu_done"), sem("hid_done")
        lg_ready, lg_done = sem("lg_ready"), sem("lg_done")
        top_done = sem("top_done")
        gap_done = sem("gap_done")
        y_ready, y_done = sem("y_ready"), sem("y_done")
        out_out = sem("out_out")
        route_exp, route = sem("route_exp"), sem("route")
        flag_turned, flag_done = sem("flag_turned"), sem("flag_done")
        e_w_in, e_z_in, e_o_in = sem("e_w_in"), sem("e_z_in"), sem("e_o_in")
        e_zT_ready, e_zT_done = sem("e_zT_ready"), sem("e_zT_done")
        e_hid_ready, e_relu_done, e_hid_done = sem("e_hid_ready"), sem("e_relu_done"), sem("e_hid_done")
        e_y_ready, e_added, e_out = sem("e_y_ready"), sem("e_added"), sem("e_out")

        STEPS = SEQS + 4
        FIRST = 5
        LAST = FIRST + (SEQS - 2 - FIRST) // 3 * 3

        def stages(t):
            return tuple(0 <= t - lag < SEQS for lag in range(5))

        def steps(eng, step):
            for t in range(FIRST):
                step(t, t % 3, stages(t), True)
            with eng.Fori(FIRST, LAST - 2, 3) as t:
                for i in range(3):
                    step(t + i if i else t, (FIRST + i) % 3, (True,) * 5, False)
            for t in range(LAST, STEPS):
                step(t, t % 3, stages(t), True)

        held = (consts_made, CONSTS)

        def each_sequence(eng, body):
            body(0)
            with eng.Fori(1, SEQS) as s:
                body(s)

        block = ctx.enter_context(nc.Block())

        @block.sync
        def _(sp):
            loads = [
                (ids_sb[:, :], ids),
                (wq_sb[:, :, :], wq.rearrange("(c p) n -> p c n", p=P)),
                (wk_sb[:, :, :], wk.rearrange("(c p) n -> p c n", p=P)),
                (wv_sb[:, :, :], wv.rearrange("(c p) n -> p c n", p=P)),
                (wo_raw[:, :, :], wo.rearrange("(c p) n -> p c n", p=P)),
                (bqk[:, 0:DC], bq.rearrange("p c -> p c")),
                (bqk[:, DC:2 * DC], bk.rearrange("p c -> p c")),
                (bv_sb[:, :], bv.partition_broadcast(P)),
                (bo_sb[:, :], bo.partition_broadcast(P)),
                (mask_sb[:, :], mask),
                (ws1_sb[:, :, :], ws1.rearrange("(c p) n -> p c n", p=P)),
                (ws2_sb[:, :], ws2),
                (wr_sb[:, :, :], wr.rearrange("(c p) n -> p c n", p=P)),
            ]
            assert len(loads) == LOADS
            for dst, src in loads:
                sp.dma_start(dst, src).then_inc(weights_in, 16)

            def carry_max(s, half, turn):
                wait(sp, max_lo, 2 * s + half + 1)
                sp.dma_start(max_dram[half].rearrange("j (r q) -> r j q", q=P), max_parts[half][:, :, :]).then_inc(max_out[half], 16)
                wait(sp, max_out[half], 16 * (s + 1))
                sp.dma_start(stack_q[turn][ROWS:SROWS, 8 * half:8 * half + 8, :],
                             max_dram[half].rearrange("j (h n) -> j h n", n=TOK)).then_inc(max_in[half], 16)

            def step(t, turn, on, edge):
                a, b, c, d, e = on
                if c:
                    carry_max(t - 2, 1, (turn - 2) % 3)
                if e:
                    wait(sp, z_done, CH * (t - 3))
                    sp.dma_start(z_dram[bass.ds(t - 4, 1), :, :].rearrange("o (c p) n -> p (o c) n", p=P), z[:, :, :]).then_inc(z_out, 16)

                def save_parts(which):
                    waits_apart(sp, held, (stacked[which], 96 * t), (part2_done, 2 * t + which + 1))
                    sp.dma_start(parts_dram[which].rearrange("k (c p) n -> p k c n", p=P),
                                 parts[:, which, :, :, :]).then_inc(parts_out[which], 16)

                def load_stack(which):
                    waits_apart(sp, held, (parts_out[which], 16 * t + 16), (t_ready, HEADS * (t - 2)))
                    for n, term in enumerate(TERMS):
                        src = parts_dram[which, term[which]].rearrange("(h d) n -> d h n", d=HD)
                        sp.dma_start(stacks[which][turn][n * HD:(n + 1) * HD, :, :], src).then_inc(stacked[which], 16)

                if a:
                    save_parts(0)
                    save_parts(1)
                    load_stack(0)
                if b:
                    carry_max(t - 1, 0, (turn - 1) % 3)
                if a:
                    load_stack(1)
                if e:
                    wait(sp, y_done, t - 3)
                    sp.dma_start(out[bass.ds(t - 4, 1), :, :].rearrange("o (c p) n -> p (o c) n", p=P), o_sb[:, :, :]).then_inc(out_out, 16)

            steps(sp, step)
            sp.wait_ge(out_out, 16 * SEQS)
            sp.wait_ge(z_out, 16 * SEQS)

        @block.gpsimd
        def _(pool):
            pool.memset(ident[:, :], 0.0).then_inc(consts_made, 1)
            pool.wait_ge(consts_made, 1)
            pool.affine_select(out=ident[:, :], in_=ident[:, :], compare_op=ALU.not_equal, fill=1.0, base=0,
                               pattern=[[-1, P]], channel_multiplier=1).then_inc(consts_made, 1)
            pool.memset(minus_half[:, :], -0.5).then_inc(consts_made, 1)
            for u in range(2):
                pool.memset(neg_max[u][:, :], 0.0).then_inc(consts_made, 1)
            for i in range(3):
                pool.memset(v[:, i, :, :, HD:2 * HD], 1.0).then_inc(consts_made, 1)
            pool.memset(any_p[:, :], 0.0).then_inc(consts_made, 1)
            pool.wait_ge(consts_made, CONSTS)
            pool.wait_ge(weights_in, 16 * LOADS)

            def gather(s, turn):
                wait(pool, x_in, 16 * CH * s)
                pool.tensor_copy(ids_now[:, :], ids_sb[:, bass.ds(CH * s, CH)]).then_inc(ids_picked, 1)
                waits_apart(pool, held, (ids_picked, s + 1), (xb_done, s - 2), (xn_done, CH * (s - 2)))
                for c in range(CH):
                    pool.indirect_dma_start(out=x[:, turn, c, :], out_offset=None, in_=emb,
                                            in_offset=bass.IndirectOffsetOnAxis(ap=ids_now[:, c:c + 1], axis=0)
                                            ).then_inc(x_in, 16)

            def rsqrt(s, mv, rs, stats, chain, used):
                waits_apart(pool, held, (stats, 2 * CH * (s + 1)), (used, CH * s))
                ve, y, yy, f, r = (rs[:, i, :] for i in range(5))
                pool.tensor_scalar(ve, mv[:, :, 1], EPS, None, ALU.add).then_inc(chain, 1)
                wait(pool, chain, 6 * s + 1)
                pool.tensor_tensor(y, ve, minus_half[:, :], ALU.pow).then_inc(chain, 1)
                wait(pool, chain, 6 * s + 2)
                pool.tensor_tensor(yy, y, y, ALU.mult).then_inc(chain, 1)
                wait(pool, chain, 6 * s + 3)
                pool.tensor_tensor(f, yy, ve, ALU.mult).then_inc(chain, 1)
                waits_apart(pool, held, (chain, 6 * s + 4))
                pool.tensor_scalar(yy, f, -0.5, 1.5, ALU.mult, ALU.add).then_inc(chain, 1)
                wait(pool, chain, 6 * s + 5)
                pool.tensor_tensor(r, y, yy, ALU.mult).then_inc(chain, 1)

            def step(t, turn, on, edge):
                a, b, c, d, e = on
                if e:
                    rsqrt(t - 4, mv2, rs2, ln2_stats, ln2_chain, z_done)
                if a:
                    for which in range(2):
                        wait(pool, part0_done, 2 * t + which + 1)
                        wait(pool, part1_done, 2 * t + which - 1)
                        wait(pool, part2_done, 2 * t + which - 1)
                        pool.tensor_tensor(qk_rest[:, which, :, :], qk[:, which, :, :], parts[:, which, 0, :, :],
                                           ALU.subtract).then_inc(rest_done, 1)
                    for which in range(2):
                        wait(pool, part1_done, 2 * t + which + 1)
                        wait(pool, parts_out[which], 16 * t)
                        wait(pool, rest_done, 2 * t + which + 1)
                        pool.tensor_tensor(parts[:, which, 2, :, :], qk_rest[:, which, :, :], parts[:, which, 1, :, :],
                                           ALU.subtract).then_inc(part2_done, 1)
                if b:
                    s = t - 1
                    wait(pool, h1_done, s - 2)
                    wait(pool, x_in, 16 * CH * (s + 1))
                    for ch in range(CH):
                        ins = pool.tensor_tensor(xb[:, (turn - 1) % 3, ch, :], x[:, (turn - 1) % 3, ch, :], bo_sb[:, :], ALU.add)
                    ins.then_inc(xb_done, 1)
                if e:
                    wait(pool, relu_done, t - 3)
                    wait(pool, y_ready, t - 4)
                    pool.tensor_tensor(hid[:, :], hid_relu[:, :], hid_relu[:, :], ALU.mult).then_inc(hid_done, 1)
                if not edge or t + 1 < SEQS:
                    rsqrt(t + 1, mv1, rs1, ln1_stats, ln1_chain, xn_done)
                if not edge or t + 2 < SEQS:
                    gather(t + 2, (turn + 2) % 3)

            gather(0, 0)
            rsqrt(0, mv1, rs1, ln1_stats, ln1_chain, xn_done)
            gather(1, 1)
            steps(pool, step)

        @block.scalar
        def _(act):
            act.wait_ge(weights_in, 16 * LOADS)
            act.wait_ge(consts_made, CONSTS)

            def first_max_part(s, half):
                wait(act, max_turned, 2 * s + half + 1)
                wait(act, max_out[half], 16 * s)
                act.activation(max_parts[half][:, 0, :], g_bank[half ^ 1][0:HEADS, 0:P], ACT.Copy).then_inc(max_hi, 1)

            def take_output(s, pair):
                wait(act, pv_ready, 4 * s + 2 * pair + 2)
                wait(act, o_ready, CH * s)
                act.activation(oT[:, 2 * pair:2 * pair + 2, :], o_bank[pair][:, :].rearrange("p (g n) -> p g n", g=2),
                               ACT.Copy).then_inc(oT_done, 1)

            def take_qk(s, which, bank):
                wait(act, (q_ready, k_ready)[which], s + 1)
                wait(act, part0_done, 2 * s + which - 1)
                wait(act, rest_done, 2 * s + which - 1)
                for ch in range(DC):
                    act.activation(qk[:, which, ch, :], bank[:, ch * TOK:(ch + 1) * TOK], ACT.Identity,
                                   bias=bqk[:, which * DC + ch:which * DC + ch + 1]).then_inc(qk_done, 1)

            def step(t, turn, on, edge):
                a, b, c, d, e = on
                for h in range(HEADS):
                    if c:
                        n = HEADS * (t - 2) + h
                        wait(act, t_ready, n + 1)
                        wait(act, pv_ready, 4 * (t - 2) + (h - 8) // GH + 1)
                        act.activation(probs[:, h % 8, :, :], t_bank[h % 2][:, :].rearrange("p (c n) -> p c n", c=CH),
                                       ACT.Exp, scale=HD ** -0.5).then_inc(exp_done, 1)
                    if h == 0 and c:
                        first_max_part(t - 2, 1)
                    if h == 1 and a:
                        wait(act, xT_ready, t + 1)
                        wait(act, v_ready, t)
                        act.activation(xT[:, :, :], g_bank[1][:, :].rearrange("p (c n) -> p c n", c=DC), ACT.Copy).then_inc(xT_done, 1)
                    if h == 1 and d:
                        take_output(t - 3, 1)
                    if h == 3 and a:
                        take_qk(t, 0, g_bank[0])
                    if h == 5 and a:
                        take_qk(t, 1, g_bank[1])
                    if h == 6 and e:
                        wait(act, zT_ready, t - 3)
                        wait(act, lg_ready, t - 4)
                        act.activation(zT[:, :, :], g_bank[0][:, :].rearrange("p (c n) -> p c n", c=DC), ACT.Copy).then_inc(zT_done, 1)
                    if h == 8 and e:
                        wait(act, hid_ready, t - 3)
                        wait(act, hid_done, t - 4)
                        act.activation(hid_relu[:, :], g_bank[0][:, 0:TOK], ACT.Relu).then_inc(relu_done, 1)
                    if h == 9 and b:
                        first_max_part(t - 1, 0)
                    if h == 10 and e:
                        wait(act, lg_ready, t - 3)
                        wait(act, gap_done, 2 * (t - 4))
                        act.activation(lg[:, :, :], g_bank[0][:, 0:CH * EXPERTS].rearrange("p (c e) -> p c e", c=CH),
                                       ACT.Copy).then_inc(lg_done, 1)
                    if h == 12 and c:
                        take_output(t - 2, 0)
                    if h == 13 and d:
                        wait(act, o_turned_ready, t - 2)
                        wait(act, h1_ready, t - 3)
                        act.activation(o_turned[:, :, :], g_bank[1][:, :].rearrange("p (c n) -> p c n", c=DC), ACT.Copy).then_inc(o_turned_done, 1)

            steps(act, step)
            act.wait_ge(gap_done, 2 * SEQS)
            act.activation(first_w[:, 0, :], gap[:, :], ACT.Exp).then_inc(route_exp, 1)

            act.wait_ge(flag_done, 1)
            flag = act.value_load(flag_i[0:1, 0:1], min_val=0, max_val=1)
            with act.If(flag > 0):
                def route_one(s):
                    act.wait_ge(e_zT_ready, s + 1)
                    act.activation(zT[:, :, :], g_bank[0][:, :].rearrange("p (c n) -> p c n", c=DC), ACT.Copy).then_inc(e_zT_done, 1)
                    for e in range(EXPERTS):
                        act.wait_ge(e_hid_ready, s * EXPERTS + (e + 1))
                        act.activation(hid_relu[:, :], g_bank[1][:, 0:TOK], ACT.Relu).then_inc(e_relu_done, 1)
                        act.wait_ge(e_relu_done, s * EXPERTS + (e + 1))
                        act.activation(hid[:, :], hid_relu[:, :], ACT.Square).then_inc(e_hid_done, 1)

                each_sequence(act, route_one)

        @block.vector
        def _(dve):
            for i in range(3):
                dve.memset(stack_k[i][ROWS:SROWS, :, :], 1.0).then_inc(ones_made, 1)
            dve.wait_ge(weights_in, 16 * LOADS)
            dve.wait_ge(consts_made, CONSTS)
            for ch in range(DC):
                dve.tensor_scalar(wo_sb[:, ch, :], wo_raw[:, ch, :], mask_sb[:, ch:ch + 1], None, ALU.mult).then_inc(wo_masked, 1)

            def statistics(src, s, stat, mv, stats, chain, before=None):
                wait(dve, chain, 6 * s)
                for ch in range(CH):
                    dve.bn_stats(stat[:, ch, :], src[:, ch, :]).then_inc(stats, 1)
                for ch in range(CH):
                    waits_apart(dve, held, (stats, 2 * CH * s + ch + 1))
                    dve.bn_aggr(mv[:, ch, :], stat[:, ch, :]).then_inc(stats, 1)

            def norm(dst, src, s, mv, rs, stats, chain, done):
                wait(dve, chain, 6 * (s + 1))
                wait(dve, stats, 2 * CH * (s + 1))
                for ch in range(CH):
                    dve.tensor_scalar(dst[:, ch, :], src[:, ch, :], mv[:, ch, 0:1], rs[:, 4, ch:ch + 1],
                                      ALU.subtract, ALU.mult).then_inc(done, 1)

            def norm_x_1(s, turn):
                wait(dve, x_in, 16 * CH * (s + 1))
                statistics(x[:, turn, :, :], s, stat1, mv1, ln1_stats, ln1_chain)

            def norm_x_2(s, turn):
                wait(dve, xT_ready, s)
                norm(xn, x[:, turn, :, :], s, mv1, rs1, ln1_stats, ln1_chain, xn_done)

            def second_max_part(s, half):
                wait(dve, max_hi, 2 * s + half + 1)
                dve.tensor_tensor(max_parts[half][:, 1, :], g_bank[half ^ 1][0:HEADS, 0:P], max_parts[half][:, 0, :],
                                  ALU.subtract).then_inc(max_lo, 1)

            def divide(s, ch):
                wait(dve, o_ready, CH * s + ch + 1)
                wait(dve, o_turned_ready, s)
                o = g_bank[1][:, :].rearrange("p (h e) -> p h e", e=2 * HD)
                dve.reciprocal(inv_sum[:, ch, :], o[:, :, HD]).then_inc(inv_done, 1)
                wait(dve, inv_done, CH * s + ch + 1)
                dve.tensor_tensor(o_nat[:, ch, :, :], o[:, :, 0:HD],
                                  inv_sum[:, ch, :].unsqueeze(2).broadcast_to([P, HEADS, HD]), ALU.mult).then_inc(o_nat_done, 1)

            def step(t, turn, on, edge):
                a, b, c, d, e = on
                for h in range(HEADS):
                    if b:
                        n = HEADS * (t - 1) + h
                        half = h // 8
                        wait(dve, s_ready, n + 1)
                        wait(dve, max_turned, 2 * (t - 1) + half - 1)
                        at = (h % 8) * CH
                        dve.tensor_reduce(neg_max[half][:, at:at + CH], s_bank[h % 2][:, :].rearrange("p (c n) -> p c n", c=CH),
                                          AX.X, ALU.max, negate=True).then_inc(max_done, 1)
                    if h == 0 and e:
                        s = t - 4
                        wait(dve, h1_ready, s + 1)
                        wait(dve, xb_done, s + 1)
                        wait(dve, y_done, s)
                        dve.tensor_tensor(h1[:, :, :], g_bank[1][:, :].rearrange("p (c n) -> p c n", c=CH),
                                          xb[:, (turn - 4) % 3, :, :], ALU.add).then_inc(h1_done, 1)
                    if h == 0 and c:
                        second_max_part(t - 2, 1)
                    if h == 1 and e:
                        wait(dve, h1_done, t - 3)
                        statistics(h1, t - 4, stat2, mv2, ln2_stats, ln2_chain)
                    if h == 3 and e:
                        wait(dve, zT_ready, t - 4)
                        wait(dve, z_out, 16 * (t - 4))
                        norm(z, h1, t - 4, mv2, rs2, ln2_stats, ln2_chain, z_done)
                    for which in range(2):
                        if h == (3, 5)[which] and a:
                            wait(dve, qk_done, 2 * DC * t + DC * (which + 1))
                            wait(dve, parts_out[which], 16 * t)
                            dve.tensor_copy(parts[:, which, 0, :, :], qk[:, which, :, :]).then_inc(part0_done, 1)
                        if h == (6, 8)[which] and a:
                            wait(dve, rest_done, 2 * t + which + 1)
                            dve.tensor_copy(parts[:, which, 1, :, :], qk_rest[:, which, :, :]).then_inc(part1_done, 1)
                    if h == 7 and d:
                        divide(t - 3, 0)
                    if h == 9 and b:
                        second_max_part(t - 1, 0)
                    if h == 10 and (not edge or t + 1 < SEQS):
                        norm_x_1(t + 1, (turn + 1) % 3)
                    if h == 11 and d:
                        divide(t - 3, 1)
                    if h == 11 and e:
                        s = t - 4
                        waits_apart(dve, held, (lg_done, s + 1), (gap_done, 2 * s))
                        for ch in range(CH):
                            dve.max(top[:, ch, :], lg[:, ch, :]).then_inc(top_done, 1)
                        dve.tensor_copy(logits[:, bass.ds(CH * s, CH), :], lg[:, :, :]).then_inc(gap_done, 1)
                        wait(dve, top_done, CH * s + CH)
                        dve.tensor_tensor(gap[:, bass.ds(CH * s, CH)], top[:, :, 1], top[:, :, 0], ALU.subtract).then_inc(gap_done, 1)
                    if h == 12 and a:
                        wait(dve, v_ready, t + 1)
                        wait(dve, pv_ready, 4 * (t - 2))
                        for ch in range(CH):
                            ins = dve.tensor_tensor(v[:, turn, ch, :, 0:HD],
                                                    g_bank[0][:, ch * D:(ch + 1) * D].rearrange("p (h e) -> p h e", e=HD),
                                                    bv_sb[:, :].rearrange("p (h e) -> p h e", e=HD), ALU.add)
                        ins.then_inc(v_done, 1)
                    if h == 13 and (not edge or t + 1 < SEQS):
                        norm_x_2(t + 1, (turn + 1) % 3)
                    if h == 14 and e:
                        wait(dve, y_ready, t - 3)
                        wait(dve, out_out, 16 * (t - 4))
                        dve.tensor_tensor(o_sb[:, :, :], g_bank[0][:, :].rearrange("p (c n) -> p c n", c=CH), h1[:, :, :],
                                          ALU.add).then_inc(y_done, 1)

            norm_x_1(0, 0)
            norm_x_2(0, 0)
            steps(dve, step)

            n = [0]

            def link(ins):
                n[0] += 1
                ins.then_inc(route, 1)
                dve.wait_ge(route, n[0])

            dve.wait_ge(route_exp, 1)
            link(dve.tensor_scalar(first_w[:, 1, :], first_w[:, 0, :], 1.0, None, ALU.add))
            link(dve.reciprocal(first_w[:, 2, :], first_w[:, 1, :]))
            link(dve.tensor_scalar(first_w[:, 3, :], first_w[:, 2, :], 1.0, None, ALU.is_ge))
            link(dve.tensor_reduce(any_p[:, 0:1], first_w[:, 3, :], AX.X, ALU.max))
            dve.wait_ge(flag_turned, 1)
            link(dve.tensor_reduce(flag_f[:, :], g_bank[0][0:1, 0:P], AX.X, ALU.max))
            dve.tensor_copy(flag_i[:, :], flag_f[:, :]).then_inc(flag_done, 1)

            dve.wait_ge(flag_done, 1)
            flag = dve.value_load(flag_i[0:1, 0:1], min_val=0, max_val=1)
            with dve.If(flag > 0):
                link(dve.tensor_reduce(best[:, :], logits[:, :, :], AX.X, ALU.max))
                link(dve.tensor_tensor(prob[:, :, :], logits[:, :, :],
                                       best[:, :].unsqueeze(2).broadcast_to([P, SEQS * CH, EXPERTS]), ALU.is_ge))
                link(dve.tensor_tensor(prob[:, :, :], prob[:, :, :],
                                       first_w[:, 3, :].unsqueeze(2).broadcast_to([P, SEQS * CH, EXPERTS]), ALU.mult))
                def route_one(s):
                    dve.wait_ge(e_o_in, s * 16 + 16)
                    for e in range(EXPERTS):
                        dve.wait_ge(e_y_ready, s * EXPERTS + (e + 1))
                        for ch in range(CH):
                            k = (s * EXPERTS + e) * CH + ch
                            if e:
                                dve.wait_ge(e_added, k - CH + 1)
                            dve.tensor_copy(top[:, ch, 0:1], prob[:, bass.ds(s * CH + ch, 1), e]).then_inc(route, 1)
                            dve.wait_ge(route, k + (ROUTE + 1))
                            dve.scalar_tensor_tensor(out=o_sb[:, ch, :], in0=g_bank[0][:, ch * D:(ch + 1) * D],
                                                     scalar=top[:, ch, 0:1], in1=o_sb[:, ch, :],
                                                     op0=ALU.mult, op1=ALU.add).then_inc(e_added, 1)

                each_sequence(dve, route_one)
            assert n[0] == ROUTE

        @block.tensor
        def _(pe):
            pe.wait_ge(weights_in, 16 * LOADS)
            pe.wait_ge(consts_made, CONSTS)
            pe.wait_ge(wo_masked, DC)
            pe.wait_ge(ones_made, 3)

            def turn_tile(bank, src, last_sem):
                for dc in range(DC):
                    for ch in range(CH):
                        at = dc * TOK + ch * P
                        ins = pe.transpose(bank[:, at:at + P], src[:, ch, dc * P:(dc + 1) * P], ident[:, :])
                ins.then_inc(last_sem, 1)

            def project_turned(bank, w, m, ready):
                for dc in range(DC):
                    ins = pe.matmul(bank[:, m * TOK:(m + 1) * TOK], w[:, dc, m * P:(m + 1) * P], xT[:, dc, :],
                                    start=(dc == 0), stop=(dc == DC - 1))
                if m == DC - 1:
                    ins.then_inc(ready, 1)

            def project(bank, src, w, ready):
                for ch in range(CH):
                    for dc in range(DC):
                        ins = pe.matmul(bank[:, ch * D:(ch + 1) * D], src[:, dc, ch * P:(ch + 1) * P], w[:, dc, :],
                                        start=(dc == 0), stop=(dc == DC - 1))
                ins.then_inc(ready, 1)

            def scores(s, h, turn):
                if h == 0:
                    for done in stacked:
                        wait(pe, done, 96 * (s + 1))
                wait(pe, max_done, HEADS * s + h - 1)
                for ch in range(CH):
                    ins = pe.matmul(s_bank[h % 2][:, ch * TOK:(ch + 1) * TOK],
                                    stack_q[turn][0:ROWS, h, ch * P:(ch + 1) * P], stack_k[turn][0:ROWS, h, :],
                                    start=True, stop=True)
                ins.then_inc(s_ready, 1)

            def scores_turned(s, h, turn):
                if h % 8 == 0:
                    wait(pe, max_in[h // 8], 16 * (s + 1))
                wait(pe, exp_done, HEADS * s + h - 1)
                for ch in range(CH):
                    ins = pe.matmul(t_bank[h % 2][:, ch * TOK:(ch + 1) * TOK],
                                    stack_k[turn][0:SROWS, h, ch * P:(ch + 1) * P], stack_q[turn][0:SROWS, h, :],
                                    start=True, stop=True)
                ins.then_inc(t_ready, 1)

            def attend(s, g, turn):
                wait(pe, exp_done, HEADS * s + GH * (g + 1))
                wait(pe, oT_done, 2 * s + g // 2 - 1)
                if g == 0:
                    wait(pe, v_done, s + 1)
                at = (g % 2) * TOK
                for ch in range(CH):
                    for i in range(GH):
                        h = GH * g + i
                        ins = pe.matmul(o_bank[g // 2][32 * i:32 * i + 32, at:at + TOK], v[:, turn, ch, h, :],
                                        probs[:, h % 8, ch, :], start=(ch == 0), stop=(ch == CH - 1),
                                        skip_group_check=True)
                ins.then_inc(pv_ready, 1)

            def turn_max(s, half):
                wait(pe, max_done, HEADS * s + 8 * (half + 1))
                pe.transpose(g_bank[half ^ 1][:, 0:P], neg_max[half][:, :], ident[:, :]).then_inc(max_turned, 1)

            def step(t, turn, on, edge):
                a, b, c, d, e = on
                if edge:
                    wait(pe, v_done, min(t, SEQS))
                    wait(pe, qk_done, 2 * DC * min(t, SEQS))
                    wait(pe, max_lo, min(2 * (t - 2) + 1, 2 * SEQS))
                    wait(pe, y_done, t - 4)
                    wait(pe, lg_done, t - 4)
                b0, b1 = g_bank
                for h in range(HEADS):
                    if b:
                        scores(t - 1, h, (turn - 1) % 3)
                    if c:
                        scores_turned(t - 2, h, (turn - 2) % 3)
                    if h == 0 and c:
                        wait(pe, y_done, t - 4)
                        turn_max(t - 2, 1)
                    if h == 1:
                        wait(pe, h1_done, t - 3)
                        if a:
                            wait(pe, xn_done, CH * (t + 1))
                            turn_tile(b1, xn, xT_ready)
                        if d:
                            attend(t - 3, 3, turn)
                    if h in (2, 3) and a:
                        wait(pe, max_lo, 2 * (t - 2) + 2)
                        wait(pe, xT_done, t + 1)
                        project_turned(b0, wq_sb, h - 2, q_ready)
                    if h in (4, 5) and a:
                        project_turned(b1, wk_sb, h - 4, k_ready)
                    if h in (5, 9, 13) and c:
                        attend(t - 2, h // GH - 1, (turn - 2) % 3)
                    if h == 6 and e:
                        if a:
                            wait(pe, qk_done, 2 * DC * t + DC)
                        elif c:
                            wait(pe, max_lo, 2 * (t - 2) + 2)
                        wait(pe, z_done, CH * (t - 3))
                        turn_tile(b0, z, zT_ready)
                    if h in (7, 11) and d:
                        ch = (h - 7) // 4
                        wait(pe, oT_done, 2 * (t - 3) + 2)
                        if ch == 0 and a:
                            wait(pe, qk_done, 2 * DC * (t + 1))
                        if ch == 1:
                            wait(pe, o_nat_done, CH * (t - 3) + 1)
                            if b:
                                wait(pe, max_lo, 2 * (t - 1) + 1)
                        for g in range(HEADS // GH):
                            ins = pe.transpose(b1[:, g * P:(g + 1) * P], oT[:, g, ch * P:(ch + 1) * P], ident[:, :])
                        ins.then_inc(o_ready, 1)
                    if h == 8 and e:
                        wait(pe, zT_done, t - 3)
                        for dc in range(DC):
                            ins = pe.matmul(b0[:, 0:TOK], ws1_sb[:, dc, :], zT[:, dc, :],
                                            start=(dc == 0), stop=(dc == DC - 1))
                        ins.then_inc(hid_ready, 1)
                    if h == 9 and b:
                        if d:
                            wait(pe, o_nat_done, CH * (t - 3) + 1)
                        elif a:
                            wait(pe, qk_done, 2 * DC * (t + 1))
                        turn_max(t - 1, 0)
                    if h == 10 and e:
                        wait(pe, relu_done, t - 3)
                        for ch in range(CH):
                            for dc in range(DC):
                                ins = pe.matmul(b0[:, ch * EXPERTS:(ch + 1) * EXPERTS], zT[:, dc, ch * P:(ch + 1) * P],
                                                wr_sb[:, dc, :], start=(dc == 0), stop=(dc == DC - 1))
                        ins.then_inc(lg_ready, 1)
                    if h == 12 and a:
                        if e:
                            wait(pe, lg_done, t - 3)
                        else:
                            wait(pe, qk_done, 2 * DC * t + DC)
                        project(b0, xT, wv_sb, v_ready)
                    if h == 13 and d:
                        wait(pe, o_nat_done, CH * (t - 2))
                        turn_tile(b1, o_nat[:, :, :, :].rearrange("p c h e -> p c (h e)"), o_turned_ready)
                    if h == 14 and e:
                        if a:
                            wait(pe, v_done, t + 1)
                        else:
                            wait(pe, lg_done, t - 3)
                        wait(pe, hid_done, t - 3)
                        for ch in range(CH):
                            ins = pe.matmul(b0[:, ch * D:(ch + 1) * D], hid[:, ch * P:(ch + 1) * P], ws2_sb[:, :],
                                            start=True, stop=True)
                        ins.then_inc(y_ready, 1)
                    if h == 15 and d:
                        wait(pe, o_turned_done, t - 2)
                        project(b1, o_turned, wo_sb, h1_ready)

            steps(pe, step)
            pe.wait_ge(lg_done, SEQS)
            pe.wait_ge(route, 4)
            pe.transpose(g_bank[0][:, 0:P], any_p[:, :], ident[:, :]).then_inc(flag_turned, 1)

            pe.wait_ge(flag_done, 1)
            flag = pe.value_load(flag_i[0:1, 0:1], min_val=0, max_val=1)
            with pe.If(flag > 0):
                pe.wait_ge(e_w_in, 16 * (DC + 1))
                def route_one(s):
                    pe.wait_ge(e_z_in, s * 16 + 16)
                    wait(pe, e_added, s * (EXPERTS * CH))
                    turn_tile(g_bank[0], z, e_zT_ready)
                    pe.wait_ge(e_zT_done, s + 1)
                    for e in range(EXPERTS):
                        wait(pe, e_relu_done, s * EXPERTS + e)
                        for dc in range(DC):
                            ins = pe.matmul(g_bank[1][:, 0:TOK], w1_sb[:, dc, e, :], zT[:, dc, :],
                                            start=(dc == 0), stop=(dc == DC - 1))
                        ins.then_inc(e_hid_ready, 1)
                        pe.wait_ge(e_hid_done, s * EXPERTS + (e + 1))
                        wait(pe, e_added, (s * EXPERTS + e) * CH)
                        for ch in range(CH):
                            ins = pe.matmul(g_bank[0][:, ch * D:(ch + 1) * D], hid[:, ch * P:(ch + 1) * P], w2_sb[:, e, :],
                                            start=True, stop=True)
                        ins.then_inc(e_y_ready, 1)

                each_sequence(pe, route_one)

        @block.sync
        def _(sp):
            sp.wait_ge(flag_done, 1)
            flag = sp.value_load(flag_i[0:1, 0:1], min_val=0, max_val=1)
            with sp.If(flag > 0):
                for ch in range(DC):
                    sp.dma_start(w1_sb[:, ch, :, :], w1[:, ch * P:(ch + 1) * P, :].rearrange("e p f -> p e f")).then_inc(e_w_in, 16)
                sp.dma_start(w2_sb[:, :, :], w2.rearrange("e f n -> f e n")).then_inc(e_w_in, 16)
                def route_one(s):
                    wait(sp, e_zT_ready, s)
                    sp.dma_start(z[:, :, :], z_dram[bass.ds(s, 1), :, :].rearrange("o (c p) n -> p (o c) n", p=P)).then_inc(e_z_in, 16)
                    wait(sp, e_out, s * 16)
                    sp.dma_start(o_sb[:, :, :], out[bass.ds(s, 1), :, :].rearrange("o (c p) n -> p (o c) n", p=P)).then_inc(e_o_in, 16)
                    sp.wait_ge(e_added, (s + 1) * (EXPERTS * CH))
                    sp.dma_start(out[bass.ds(s, 1), :, :].rearrange("o (c p) n -> p (o c) n", p=P), o_sb[:, :, :]).then_inc(e_out, 16)

                each_sequence(sp, route_one)
                sp.wait_ge(e_out, SEQS * 16)


LOADS = 13
CONSTS = 9
ROUTE = 8


_ORDER = ["ids", "emb", "wq", "bq", "wk", "bk", "wv", "bv", "wo", "bo", "mask", "ws1", "ws2", "w1", "w2", "wr"]


def kernel(x, L0_tok_embeddings, L0_attn_Wq, L0_attn_bq, L0_attn_Wk, L0_attn_bk, L0_attn_Wv, L0_attn_bv,
           L0_attn_Wo, L0_attn_bo, L0_attn_head_mask, L0_ffn_Ws1, L0_ffn_Ws2, L0_ffn_W1, L0_ffn_W2, L0_ffn_Wr):
    import numpy as np
    import concourse.bacc as bacc
    from concourse import mybir as mb
    from concourse.bass_utils import run_bass_kernel_spmd

    seqs, tok = x.shape
    d = L0_tok_embeddings.shape[1]
    heads = L0_attn_head_mask.shape[0]
    c = np.ascontiguousarray
    data = {
        "ids": c(np.asarray(x).reshape(-1, 128).T),
        "emb": c(np.asarray(L0_tok_embeddings)),
        "wq": c(np.asarray(L0_attn_Wq).T), "wk": c(np.asarray(L0_attn_Wk).T),
        "wv": c(np.asarray(L0_attn_Wv).T), "wo": c(np.asarray(L0_attn_Wo).T),
        "bq": c(np.asarray(L0_attn_bq).reshape(-1, 128).T), "bk": c(np.asarray(L0_attn_bk).reshape(-1, 128).T),
        "bv": c(np.asarray(L0_attn_bv)), "bo": c(np.asarray(L0_attn_bo)),
        "mask": c(np.repeat(np.asarray(L0_attn_head_mask), d // heads).reshape(-1, 128).T),
        "ws1": c(np.asarray(L0_ffn_Ws1)), "ws2": c(np.asarray(L0_ffn_Ws2)),
        "w1": c(np.asarray(L0_ffn_W1)), "w2": c(np.asarray(L0_ffn_W2)), "wr": c(np.asarray(L0_ffn_Wr)),
    }
    nc = bacc.Bacc("TRN2", target_bir_lowering=False, num_devices=1)
    arrays, args = {}, []
    for name in _ORDER:
        arrays[f"in_{name}"] = data[name]
        args.append(nc.dram_tensor(f"in_{name}", data[name].shape, mb.dt.from_np(data[name].dtype), kind="ExternalInput").ap())
    out = nc.dram_tensor("out_0", (seqs, tok, d), mb.dt.float32, kind="ExternalOutput").ap()
    tower(nc, *args, out)
    r = run_bass_kernel_spmd(nc, [arrays], core_ids=[0])
    return r.results[0]["out_0"]
```

```python
import concourse.bass as bass
from concourse import mybir
from contextlib import ExitStack

F32 = mybir.dt.float32
F32R = mybir.dt.float32r
BF16 = mybir.dt.bfloat16
I32 = mybir.dt.int32
ALU = mybir.AluOpType
ACT = mybir.ActivationFunctionType
AX = mybir.AxisListType

P = 128
TERMS = [(0, 0), (0, 1), (0, 2), (1, 0), (1, 1), (2, 0)]
PIECES = (3, 2, 1)
EPS = 1e-5


def wait(eng, sem, value):
    if not isinstance(value, int) or value > 0:
        eng.wait_ge(sem, value)


def waits_apart(eng, held, *waits):
    if all(isinstance(value, int) for _, value in waits):
        for sem, value in waits:
            wait(eng, sem, value)
    else:
        waits = [(sem, eng.to_reg(value)) for sem, value in waits]
        eng.wait_ge(*held)
        for sem, value in waits:
            eng.wait_ge(sem, value)


def tower(nc, ids, emb, wq, bq, wk, bk, wv, bv, wo, bo, mask, ws1, ws2, w1, w2, wr, out):
    SEQS, TOK, D = out.shape
    HEADS = 16
    HD = D // HEADS
    CH = TOK // P
    DC = D // P
    HC = P // HD
    GH = 4
    F = ws1.shape[1]
    EXPERTS = wr.shape[1]
    ROWS = len(TERMS) * HD
    SROWS = ROWS + 2
    W = DC * TOK

    ctx = ExitStack()
    with ctx:
        def sb(name, shape, dt=F32):
            return ctx.enter_context(nc.sbuf_tensor(name, shape, dt))

        def bank(name):
            return ctx.enter_context(nc.psum_tensor(name, [P, W], F32))

        def sem(name):
            return ctx.enter_context(nc.semaphore(name))

        parts_dram = nc.dram_tensor("parts_dram", [2, 3, D, TOK], BF16, kind="Internal").ap()
        max_dram = nc.dram_tensor("max_dram", [2, 2, HEADS // 2 * TOK], BF16, kind="Internal").ap()
        sums_dram = nc.dram_tensor("sums_dram", [2, GH, DC * TOK], F32, kind="Internal").ap()
        inv_dram = nc.dram_tensor("inv_dram", [2 * GH, DC * TOK], F32, kind="Internal").ap()
        o_dram = nc.dram_tensor("o_dram", [2, GH, HD, DC * TOK], F32, kind="Internal").ap()
        z_dram = nc.dram_tensor("z_dram", [SEQS, TOK, D], F32, kind="Internal").ap()

        ident = sb("ident", [P, P])
        ids_sb = sb("ids_sb", [P, SEQS * CH], I32)
        ids_now = sb("ids_now", [P, CH], I32)
        wq_sb, wk_sb, wv_sb, wo_sb, wo_raw = (sb(n, [P, DC, D]) for n in ("wq_sb", "wk_sb", "wv_sb", "wo_sb", "wo_raw"))

        def halves(name, shape):
            return sb(name + "_hi", shape, F32R), sb(name + "_lo", shape, F32R)

        wq_2, wk_2, wv_2, wo_2 = (halves(n, [P, DC, D]) for n in ("wq", "wk", "wv", "wo"))
        bqk = sb("bqk", [P, 2 * DC])
        bv_sb = sb("bv_sb", [P, D])
        bo_sb = sb("bo_sb", [P, D])
        mask_sb = sb("mask_sb", [P, DC])
        ws1_sb = sb("ws1_sb", [P, DC, F])
        ws2_sb = sb("ws2_sb", [P, D])
        wr_sb = sb("wr_sb", [P, 3, DC, P])
        ws1_2, ws2_2, wr_2 = halves("ws1", [P, DC, F]), halves("ws2", [P, D]), halves("wr", [P, 3, DC, P])
        minus_half = sb("minus_half", [P, 2 * CH])

        x = sb("x", [P, 3, CH, D])
        stat1 = sb("stat1", [P, CH, 6])
        mv = sb("mv", [P, 2 * CH, 2])
        rs = sb("rs", [P, 5, 2 * CH])
        xn = sb("xn", [P, CH, D])
        xT_2 = halves("xT", [P, DC, TOK])
        qk = sb("qk", [P, 2, DC, TOK])
        qk_rest = sb("qk_rest", [P, 2, DC, TOK])
        parts = sb("parts", [P, 2, 3, DC, TOK], BF16)
        stack_q = [sb(f"stack_q{i}", [P, HEADS, TOK], BF16) for i in range(3)]
        stack_k = [sb(f"stack_k{i}", [P, HEADS, TOK], BF16) for i in range(3)]
        stacks = (stack_q, stack_k)
        v = sb("v", [P, 3, CH, HEADS, 2 * HD])
        neg_max = [sb(f"neg_max{u}", [P, P]) for u in range(2)]
        max_parts = [sb(f"max_parts{u}", [HEADS, 2, P], BF16) for u in range(2)]
        probs = sb("probs", [P, 8, CH, TOK])
        oT = sb("oT", [P, 2, DC, TOK])
        sums = sb("sums", [P, HEADS * TOK // P])
        inv_sums = sb("inv_sums", [P, HEADS * TOK // P])
        inv_wide = sb("inv_wide", [P, DC, TOK])
        o_packed = sb("o_packed", [P, DC, TOK])
        o_turned = sb("o_turned", [P, DC, TOK])
        o_2 = halves("o", [P, DC, TOK])
        xb = sb("xb", [P, 3, CH, D])
        h1 = sb("h1", [P, CH, D])
        stat2 = sb("stat2", [P, CH, 6])
        z = sb("z", [P, CH, D])
        zT_2 = halves("zT", [P, DC, TOK])
        zT = sb("zT", [P, DC, TOK])
        hid_relu = sb("hid_relu", [P, TOK])
        hid = sb("hid", [P, TOK])
        hid_2 = halves("hid", [P, TOK])
        lgT = sb("lgT", [P, TOK])
        top = sb("top", [P, 3, CH, 8])
        weight = sb("weight", [P, CH])
        o_sb = sb("o_sb", [P, CH, D])
        logits = sb("logits", [P, SEQS * CH, EXPERTS])
        gap = sb("gap", [P, SEQS * CH])
        first_w = sb("first_w", [P, 4, SEQS * CH])
        best = sb("best", [P, SEQS * CH])
        prob = sb("prob", [P, SEQS * CH, EXPERTS])
        any_p = sb("any_p", [P, P])
        flag_f = sb("flag_f", [1, 1])
        flag_i = sb("flag_i", [1, 1], I32)
        half_probs = [probs[:, i:i + 4, :, :].rearrange("p b c n -> p (b c n)") for i in (0, 4)]
        w1_sb = half_probs[0].rearrange("p (c e f) -> p c e f", c=DC, e=EXPERTS)
        w2_sb = half_probs[1].rearrange("p (e n) -> p e n", e=EXPERTS)

        s_bank = [bank(f"s_bank{i}") for i in range(2)]
        t_bank = [bank(f"t_bank{i}") for i in range(2)]
        o_bank = [bank(f"o_bank{i}") for i in range(2)]
        g_bank = [bank(f"g_bank{i}") for i in range(2)]

        ids_in, qkv_in = sem("ids_in"), sem("qkv_in")
        weights_in = sem("weights_in")
        consts_made = sem("consts_made")
        ones_made, v_ones_made = sem("ones_made"), sem("v_ones_made")
        zeros_made = sem("zeros_made")
        wo_masked = sem("wo_masked")
        qkv_hi, qkv_lo = sem("qkv_hi"), sem("qkv_lo")
        w_hi, w_lo = sem("w_hi"), sem("w_lo")
        ids_picked = sem("ids_picked")
        x_in = sem("x_in")
        xb_done = sem("xb_done")
        ln1_stats = sem("ln1_stats")
        ln_chain = sem("ln_chain")
        xn_done = sem("xn_done")
        xT_ready = sem("xT_ready")
        xT_hi, xT_lo = sem("xT_hi_done"), sem("xT_lo_done")
        q_ready, k_ready, v_ready = sem("q_ready"), sem("k_ready"), sem("v_ready")
        qk_done = sem("qk_done")
        part0_done = sem("part0_done")
        rest_done = [sem("q_rest_done"), sem("k_rest_done")]
        part1_done = sem("part1_done")
        part2_done = sem("part2_done")
        parts_out = [sem("q_parts_out"), sem("k_parts_out")]
        stacked = [sem("q_stacked"), sem("k_stacked")]
        v_done = sem("v_done")
        s_ready, max_done = sem("s_ready"), sem("max_done")
        max_turned = sem("max_turned")
        max_hi, max_lo = sem("max_hi"), sem("max_lo")
        max_in = [sem("max_in0"), sem("max_in1")]
        max_out = [sem("max_out0"), sem("max_out1")]
        t_ready, exp_done = sem("t_ready"), sem("exp_done")
        pv_ready = sem("pv_ready")
        oT_done = sem("oT_done")
        sums_out, o_out = sem("sums_out"), sem("o_out")
        sums_in, inv_done = sem("sums_in"), sem("inv_done")
        inv_out, inv_in = sem("inv_out"), sem("inv_in")
        o_in = sem("o_in")
        o_turned_done = sem("o_turned_done")
        o_hi, o_lo = sem("o_hi_done"), sem("o_lo_done")
        h1_ready, h1_done = sem("h1_ready"), sem("h1_done")
        ln2_stats = sem("ln2_stats")
        z_done = sem("z_done")
        z_out = sem("z_out")
        zT_ready, zT_hi, zT_lo = sem("zT_ready"), sem("zT_hi_done"), sem("zT_lo_done")
        hid_ready, relu_done, hid_done = sem("hid_ready"), sem("relu_done"), sem("hid_done")
        hid_hi, hid_lo = sem("hid_hi_done"), sem("hid_lo_done")
        lg_ready, lg_done = sem("lg_ready"), sem("lg_done")
        lg_turned, lg_kept, gap_done = sem("lg_turned"), sem("lg_kept"), sem("gap_done")
        top_done = sem("top_done")
        y_ready, y_done = sem("y_ready"), sem("y_done")
        out_out = sem("out_out")
        route_exp, route = sem("route_exp"), sem("route")
        flag_turned, flag_done = sem("flag_turned"), sem("flag_done")
        e_w_in, e_z_in, e_o_in = sem("e_w_in"), sem("e_z_in"), sem("e_o_in")
        e_zT_ready, e_zT_done = sem("e_zT_ready"), sem("e_zT_done")
        e_hid_ready, e_relu_done, e_hid_done = sem("e_hid_ready"), sem("e_relu_done"), sem("e_hid_done")
        e_y_ready, e_added, e_out = sem("e_y_ready"), sem("e_added"), sem("e_out")

        STEPS = SEQS + 4
        FIRST = 5
        LAST = FIRST + (SEQS - 2 - FIRST) // 3 * 3

        def stages(t):
            return tuple(0 <= t - lag < SEQS for lag in range(5))

        def steps(eng, step):
            for t in range(FIRST):
                step(t, t % 3, stages(t), True)
            with eng.Fori(FIRST, LAST - 2, 3) as t:
                for i in range(3):
                    step(t + i if i else t, (FIRST + i) % 3, (True,) * 5, False)
            for t in range(LAST, STEPS):
                step(t, t % 3, stages(t), True)

        held = (consts_made, CONSTS)

        def each_sequence(eng, body):
            body(0)
            with eng.Fori(1, SEQS) as s:
                body(s)

        def load_max(eng, s, half, turn):
            wait(eng, max_out[half], 16 * (s + 1))
            eng.dma_start(stack_q[turn][ROWS:SROWS, 8 * half:8 * half + 8, :],
                         max_dram[half].rearrange("j (h n) -> j h n", n=TOK)).then_inc(max_in[half], 16)

        block = ctx.enter_context(nc.Block())

        @block.sync
        def _(sp):
            chunks = "(c p) n -> p c n"
            sp.dma_start(ids_sb[:, :], ids).then_inc(ids_in, 16)
            sp.dma_start(wq_sb[:, :, :], wq.rearrange(chunks, p=P)).then_inc(qkv_in, 16)
            sp.dma_start(wk_sb[:, :, :], wk.rearrange(chunks, p=P)).then_inc(qkv_in, 16)
            sp.dma_start(bqk[:, 0:DC], bq).then_inc(qkv_in, 16)
            sp.dma_start(bqk[:, DC:2 * DC], bk).then_inc(qkv_in, 16)
            sp.dma_start(wv_sb[:, :, :], wv.rearrange(chunks, p=P)).then_inc(qkv_in, 16)
            sp.dma_start(bv_sb[:, :], bv.partition_broadcast(P)).then_inc(qkv_in, 16)
            sp.dma_start(bo_sb[:, :], bo.partition_broadcast(P)).then_inc(weights_in, 16)
            sp.dma_start(wo_raw[:, :, :], wo.rearrange(chunks, p=P)).then_inc(weights_in, 16)
            sp.dma_start(mask_sb[:, :], mask).then_inc(weights_in, 16)
            sp.dma_start(ws1_sb[:, :, :], ws1.rearrange(chunks, p=P)).then_inc(weights_in, 16)
            sp.dma_start(ws2_sb[:, :], ws2).then_inc(weights_in, 16)
            sp.wait_ge(zeros_made, 2)
            for j in range(3):
                sp.dma_start(wr_sb[:, j, :, 32 * j:32 * j + EXPERTS], wr.rearrange(chunks, p=P)).then_inc(weights_in, 16)

            def step(t, turn, on, edge):
                a, b, c, d, e = on
                if d:
                    s = t - 3
                    waits_apart(sp, held, (oT_done, 2 * s + 2), (sums_in, 16 * s), (o_in, 16 * s))
                    sp.dma_start(sums_dram.rearrange("g i n -> i g n"),
                                 oT[HD::P // GH, :, :, :].rearrange("i g c n -> i g (c n)")).then_inc(sums_out, 16)
                    for i in range(GH):
                        rows = P // GH * i
                        sp.dma_start(o_dram[:, i, :, :].rearrange("g r n -> r g n"),
                                     oT[rows:rows + HD, :, :, :].rearrange("r g c n -> r g (c n)")).then_inc(o_out, 16)
                if d:
                    waits_apart(sp, held, (sums_out, 16 * s + 16), (inv_done, s))
                    sp.dma_start(sums[:, :], sums_dram.rearrange("g i (k n) -> (g i k) n", n=HEADS * TOK // P)).then_inc(sums_in, 16)
                if e:
                    wait(sp, z_done, CH * (t - 3))
                    sp.dma_start(z_dram[bass.ds(t - 4, 1), :, :].rearrange("o (c p) n -> p (o c) n", p=P), z[:, :, :]).then_inc(z_out, 16)
                if d:
                    waits_apart(sp, held, (o_out, GH * 16 * s + GH * 16), (o_turned_done, s))
                    sp.dma_start(o_packed[:, :, :].rearrange("p c n -> p (c n)"), o_dram.rearrange("g i r n -> (g i r) n")).then_inc(o_in, 16)
                    waits_apart(sp, held, (inv_done, s + 1), (inv_in, 16 * s))
                    sp.dma_start(inv_dram.rearrange("k (m n) -> (k m) n", n=HEADS * TOK // P), inv_sums[:, :]).then_inc(inv_out, 16)

                def save_parts(which):
                    waits_apart(sp, held, (stacked[which], 16 * len(PIECES) * t), (part2_done, 2 * t + which + 1))
                    sp.dma_start(parts_dram[which].rearrange("k (c p) n -> p k c n", p=P),
                                 parts[:, which, :, :, :]).then_inc(parts_out[which], 16)

                def load_stack(which):
                    waits_apart(sp, held, (parts_out[which], 16 * t + 16), (t_ready, HEADS * (t - 2)))
                    src = parts_dram[which].rearrange("k (d h) n -> d k (h n)", d=HD)
                    dst = stacks[which][turn][:, :, :].rearrange("r h n -> r (h n)")
                    row = 0
                    for part, terms in enumerate(PIECES):
                        rows = src[:, part:part + 1, :].broadcast_to([HD, terms, HEADS * TOK]) if which == 0 else src[:, 0:terms, :]
                        sp.dma_start(dst[row:row + terms * HD, :], rows).then_inc(stacked[which], 16)
                        row += terms * HD

                if a:
                    save_parts(0)
                if d:
                    wait(sp, inv_out, 16 * (s + 1))
                    sp.dma_start(inv_wide[:, :, :].rearrange("p c n -> p (c n)"),
                                 inv_dram.unsqueeze(1).broadcast_to([2 * GH, HD, DC * TOK])).then_inc(inv_in, 16)
                if a:
                    save_parts(1)
                if a:
                    load_stack(0)
                if a:
                    load_stack(1)
                if b:
                    load_max(sp, t - 1, 0, (turn - 1) % 3)
                if e:
                    wait(sp, y_done, t - 3)
                    sp.dma_start(out[bass.ds(t - 4, 1), :, :].rearrange("o (c p) n -> p (o c) n", p=P), o_sb[:, :, :]).then_inc(out_out, 16)

            steps(sp, step)
            sp.wait_ge(out_out, 16 * SEQS)
            sp.wait_ge(z_out, 16 * SEQS)

        @block.gpsimd
        def _(pool):
            def constants():
                pool.memset(ident[:, :], 0.0).then_inc(consts_made, 1)
                pool.wait_ge(consts_made, 1)
                pool.affine_select(out=ident[:, :], in_=ident[:, :], compare_op=ALU.not_equal, fill=1.0, base=0,
                                   pattern=[[-1, P]], channel_multiplier=1).then_inc(consts_made, 1)
                pool.memset(minus_half[:, :], -0.5).then_inc(consts_made, 1)
                pool.wait_ge(consts_made, CONSTS)

            def zeros():
                pool.memset(any_p[:, :], 0.0).then_inc(zeros_made, 1)
                pool.memset(wr_sb[:, :, :, :], 0.0).then_inc(zeros_made, 1)
                for u in range(2):
                    pool.memset(neg_max[u][:, :], 0.0).then_inc(zeros_made, 1)
                pool.memset(lgT[:, :], 0.0).then_inc(zeros_made, 1)

            def gather(s, turn):
                wait(pool, x_in, 16 * CH * s)
                pool.tensor_copy(ids_now[:, :], ids_sb[:, bass.ds(CH * s, CH)]).then_inc(ids_picked, 1)
                waits_apart(pool, held, (ids_picked, s + 1), (xb_done, s - 2), (xn_done, CH * (s - 2)))
                for c in range(CH):
                    pool.indirect_dma_start(out=x[:, turn, c, :], out_offset=None, in_=emb,
                                            in_offset=bass.IndirectOffsetOnAxis(ap=ids_now[:, c:c + 1], axis=0)
                                            ).then_inc(x_in, 16)

            def rsqrt(t, of_x, of_h1):
                n = 6 * (t + 1)
                waits = [(ln1_stats, 2 * CH * (t + 2))] if of_x else []
                waits += [(ln2_stats, 2 * CH * (t - 3))] if of_h1 else []
                waits_apart(pool, held, *waits)
                now = slice(0 if of_x else CH, 2 * CH if of_h1 else CH)
                ve, y, yy, f, r = (rs[:, i, now] for i in range(5))
                pool.tensor_scalar(ve, mv[:, now, 1], EPS, None, ALU.add).then_inc(ln_chain, 1)
                wait(pool, ln_chain, n + 1)
                pool.tensor_tensor(y, ve, minus_half[:, now], ALU.pow).then_inc(ln_chain, 1)
                wait(pool, ln_chain, n + 2)
                pool.tensor_tensor(yy, y, y, ALU.mult).then_inc(ln_chain, 1)
                wait(pool, ln_chain, n + 3)
                pool.tensor_tensor(f, yy, ve, ALU.mult).then_inc(ln_chain, 1)
                waits_apart(pool, held, (ln_chain, n + 4))
                pool.tensor_scalar(yy, f, -0.5, 1.5, ALU.mult, ALU.add).then_inc(ln_chain, 1)
                wait(pool, ln_chain, n + 5)
                pool.tensor_tensor(r, y, yy, ALU.mult).then_inc(ln_chain, 1)

            def third_part(t, which):
                wait(pool, part1_done, 2 * t + which + 1)
                wait(pool, parts_out[which], 16 * t)
                wait(pool, rest_done[which], t + 1)
                pool.tensor_tensor(parts[:, which, 2, :, :], qk_rest[:, which, :, :], parts[:, which, 1, :, :],
                                   ALU.subtract).then_inc(part2_done, 1)

            def step(t, turn, on, edge):
                a, b, c, d, e = on
                if b:
                    s = t - 1
                    if edge and t == 1:
                        pool.wait_ge(weights_in, 16 * WEIGHTS)
                    wait(pool, h1_done, s - 2)
                    wait(pool, x_in, 16 * CH * (s + 1))
                    for ch in range(CH):
                        ins = pool.tensor_tensor(xb[:, (turn - 1) % 3, ch, :], x[:, (turn - 1) % 3, ch, :], bo_sb[:, :], ALU.add)
                    ins.then_inc(xb_done, 1)
                rsqrt(t, not edge or t + 1 < SEQS, e)
                if not edge or t + 2 < SEQS:
                    gather(t + 2, (turn + 2) % 3)
                if a:
                    third_part(t, 0)
                    third_part(t, 1)
                if edge and t == 0:
                    pool.wait_ge(part2_done, 2)
                    for i in range(1, 3):
                        pool.memset(stack_k[i][ROWS:SROWS, :, :], 1.0).then_inc(ones_made, 1)
                    pool.wait_ge(ones_made, 3)
                if e:
                    wait(pool, relu_done, t - 3)
                    wait(pool, hid_lo, t - 4)
                    pool.tensor_tensor(hid[:, :], hid_relu[:, :], hid_relu[:, :], ALU.mult).then_inc(hid_done, 1)
                if d:
                    s = t - 3
                    wait(pool, inv_in, 16 * (s + 1))
                    wait(pool, o_in, 16 * (s + 1))
                    wait(pool, o_hi, s)
                    pool.tensor_tensor(o_turned[:, :, :], o_packed[:, :, :], inv_wide[:, :, :], ALU.mult).then_inc(o_turned_done, 1)
                if e:
                    wait(pool, hid_hi, t - 3)
                    wait(pool, hid_done, t - 3)
                    wait(pool, y_ready, t - 4)
                    pool.tensor_tensor(hid_2[1][:, :], hid[:, :], hid_2[0][:, :].bitcast(F32), ALU.subtract).then_inc(hid_lo, 1)
                if d:
                    wait(pool, o_hi, t - 2)
                    wait(pool, o_turned_done, t - 2)
                    wait(pool, h1_ready, t - 3)
                    pool.tensor_tensor(o_2[1][:, :, :], o_turned[:, :, :], o_2[0][:, :, :].bitcast(F32), ALU.subtract).then_inc(o_lo, 1)

            constants()
            pool.wait_ge(ids_in, 16)
            gather(0, 0)
            zeros()
            rsqrt(-1, True, False)
            gather(1, 1)
            steps(pool, step)

        @block.scalar
        def _(act):
            act.wait_ge(qkv_in, 16 * QKV)
            act.wait_ge(consts_made, CONSTS)
            for w, w_2 in ((wq_sb, wq_2), (wk_sb, wk_2), (wv_sb, wv_2)):
                act.activation(w_2[0][:, :, :], w[:, :, :], ACT.Copy).then_inc(qkv_hi, 1)

            def first_max_part(s, half):
                wait(act, max_turned, 2 * s + half + 1)
                wait(act, max_out[half], 16 * s)
                act.activation(max_parts[half][:, 0, :], g_bank[1][0:HEADS, 0:P], ACT.Copy).then_inc(max_hi, 1)

            def save_max(s, half):
                wait(act, max_lo, 2 * s + half + 1)
                act.dma_start(max_dram[half].rearrange("j (r q) -> r j q", q=P), max_parts[half][:, :, :]).then_inc(max_out[half], 16)

            def take_output(s, pair):
                wait(act, pv_ready, 4 * s + 2 * pair + 2)
                wait(act, sums_out, 16 * s)
                wait(act, o_out, GH * 16 * s)
                act.activation(oT[:, :, pair, :], o_bank[pair][:, :].rearrange("p (g n) -> p g n", g=2),
                               ACT.Copy).then_inc(oT_done, 1)

            def take_qk(s, which, bank):
                wait(act, (q_ready, k_ready)[which], s + 1)
                wait(act, rest_done[which], s)
                wait(act, part2_done, 2 * s + which - 1)
                wait(act, parts_out[which], 16 * s)
                for ch in range(DC):
                    for dst, done in ((qk[:, which, ch, :], qk_done), (parts[:, which, 0, ch, :], part0_done)):
                        act.activation(dst, bank[:, ch * TOK:(ch + 1) * TOK], ACT.Identity,
                                       bias=bqk[:, which * DC + ch:which * DC + ch + 1]).then_inc(done, 1)

            def step(t, turn, on, edge):
                a, b, c, d, e = on
                if edge and t == 1:
                    act.wait_ge(wo_masked, DC)
                    act.activation(wo_2[0][:, :, :], wo_sb[:, :, :], ACT.Copy).then_inc(w_hi, 1)
                    act.activation(ws1_2[0][:, :, :], ws1_sb[:, :, :], ACT.Copy).then_inc(w_hi, 1)
                    act.activation(ws2_2[0][:, :], ws2_sb[:, :], ACT.Copy).then_inc(w_hi, 1)
                    act.activation(wr_2[0][:, :, :, :], wr_sb[:, :, :, :], ACT.Copy).then_inc(w_hi, 1)
                for h in range(HEADS):
                    if h == 0 and a:
                        wait(act, xT_ready, t + 1)
                        wait(act, v_ready, t)
                        act.activation(xT_2[0][:, :, :], g_bank[0][:, :].rearrange("p (c n) -> p c n", c=DC), ACT.Copy).then_inc(xT_hi, 1)
                    if h == 2 and c:
                        first_max_part(t - 2, 1)
                    if h == 11 and b:
                        first_max_part(t - 1, 0)
                    if h == 12 and b:
                        save_max(t - 1, 0)
                    if h == 12 and d:
                        wait(act, o_turned_done, t - 2)
                        wait(act, h1_ready, t - 3)
                        wait(act, o_lo, t - 3)
                        act.activation(o_2[0][:, :, :], o_turned[:, :, :], ACT.Copy).then_inc(o_hi, 1)
                    if c:
                        n = HEADS * (t - 2) + h
                        wait(act, t_ready, n + 1)
                        wait(act, pv_ready, 4 * (t - 2) + (h - 8) // GH + 1)
                        act.activation(probs[:, h % 8, :, :], t_bank[h % 2][:, :].rearrange("p (c n) -> p c n", c=CH),
                                       ACT.Exp, scale=HD ** -0.5).then_inc(exp_done, 1)
                    if h == 1 and d:
                        take_output(t - 3, 1)
                    if h == 3 and a:
                        take_qk(t, 0, g_bank[0])
                    if h == 5 and a:
                        take_qk(t, 1, g_bank[1])
                    if h == 6 and e:
                        wait(act, zT_ready, t - 3)
                        wait(act, lg_ready, t - 4)
                        act.activation(zT_2[0][:, :, :], g_bank[0][:, :].rearrange("p (c n) -> p c n", c=DC), ACT.Copy).then_inc(zT_hi, 1)
                    if h == 10 and e:
                        wait(act, hid_ready, t - 3)
                        wait(act, hid_done, t - 4)
                        act.activation(hid_relu[:, :], g_bank[0][:, 0:TOK], ACT.Relu).then_inc(relu_done, 1)
                        wait(act, relu_done, t - 3)
                        wait(act, y_ready, t - 4)
                        wait(act, hid_lo, t - 4)
                        act.activation(hid_2[0][:, :], hid_relu[:, :], ACT.Square).then_inc(hid_hi, 1)
                    if h == 11 and e:
                        wait(act, lg_ready, t - 3)
                        at = 32 * ((turn + 1) % 3)
                        if edge and t == 4:
                            act.wait_ge(zeros_made, ZEROS)
                        if turn == 2:
                            wait(act, lg_turned, t - 2)
                        act.activation(lgT[at:at + 32, :], g_bank[0][at:at + 32, 0:TOK], ACT.Copy).then_inc(lg_done, 1)
                    if h == 3 and c:
                        save_max(t - 2, 1)
                    if h == 5 and c:
                        load_max(act, t - 2, 1, (turn - 2) % 3)
                    if h == 12 and c:
                        take_output(t - 2, 0)

            steps(act, step)
            act.wait_ge(gap_done, SEQS + 2)
            act.activation(first_w[:, 0, :], gap[:, :], ACT.Exp).then_inc(route_exp, 1)

            act.wait_ge(flag_done, 1)
            flag = act.value_load(flag_i[0:1, 0:1], min_val=0, max_val=1)
            with act.If(flag > 0):
                def route_one(s):
                    act.wait_ge(e_zT_ready, s + 1)
                    act.activation(zT[:, :, :], g_bank[0][:, :].rearrange("p (c n) -> p c n", c=DC), ACT.Copy).then_inc(e_zT_done, 1)
                    for e in range(EXPERTS):
                        act.wait_ge(e_hid_ready, s * EXPERTS + (e + 1))
                        act.activation(hid_relu[:, :], g_bank[1][:, 0:TOK], ACT.Relu).then_inc(e_relu_done, 1)
                        act.wait_ge(e_relu_done, s * EXPERTS + (e + 1))
                        act.activation(hid[:, :], hid_relu[:, :], ACT.Square).then_inc(e_hid_done, 1)

                each_sequence(act, route_one)

        @block.vector
        def _(dve):
            for i in range(3):
                dve.memset(v[:, i, :, :, HD:2 * HD], 1.0).then_inc(v_ones_made, 1)
            dve.memset(stack_k[0][ROWS:SROWS, :, :], 1.0).then_inc(ones_made, 1)
            dve.wait_ge(consts_made, CONSTS)

            def statistics(src, s, stat, at, stats, chain):
                wait(dve, ln_chain, chain)
                for ch in range(CH):
                    dve.bn_stats(stat[:, ch, :], src[:, ch, :]).then_inc(stats, 1)
                for ch in range(CH):
                    waits_apart(dve, held, (stats, 2 * CH * s + ch + 1))
                    dve.bn_aggr(mv[:, at + ch, :], stat[:, ch, :]).then_inc(stats, 1)

            def rest(t, which):
                wait(dve, qk_done, 2 * DC * t + DC * (which + 1))
                wait(dve, part0_done, 2 * DC * t + DC * (which + 1))
                wait(dve, part1_done, 2 * t + which - 1)
                wait(dve, part2_done, 2 * t + which - 1)
                dve.tensor_tensor(qk_rest[:, which, :, :], qk[:, which, :, :], parts[:, which, 0, :, :],
                                   ALU.subtract).then_inc(rest_done[which], 1)

            def norm(dst, src, s, at, stats, chain, done):
                wait(dve, ln_chain, chain)
                wait(dve, stats, 2 * CH * (s + 1))
                for ch in range(CH):
                    dve.tensor_scalar(dst[:, ch, :], src[:, ch, :], mv[:, at + ch, 0:1], rs[:, 4, at + ch:at + ch + 1],
                                      ALU.subtract, ALU.mult).then_inc(done, 1)

            def norm_x_1(s, turn):
                wait(dve, x_in, 16 * CH * (s + 1))
                statistics(x[:, turn, :, :], s, stat1, 0, ln1_stats, 6 * s)

            def norm_x_2(s, turn):
                wait(dve, xT_ready, s)
                norm(xn, x[:, turn, :, :], s, 0, ln1_stats, 6 * (s + 1), xn_done)

            def second_max_part(s, half):
                wait(dve, max_hi, 2 * s + half + 1)
                dve.tensor_tensor(max_parts[half][:, 1, :], g_bank[1][0:HEADS, 0:P], max_parts[half][:, 0, :],
                                  ALU.subtract).then_inc(max_lo, 1)

            def step(t, turn, on, edge):
                a, b, c, d, e = on
                if edge and t == 2:
                    dve.wait_ge(w_hi, 4)
                    for w, (hi, lo) in ((wo_sb[:, :, :], (x[:, :, :] for x in wo_2)), (ws1_sb[:, :, :], (x[:, :, :] for x in ws1_2)),
                                        (ws2_sb[:, :], (x[:, :] for x in ws2_2)),
                                        (wr_sb[:, :, :, :].rearrange("p j c n -> p (j c n)"),
                                         (x[:, :, :, :].rearrange("p j c n -> p (j c n)") for x in wr_2))):
                        dve.tensor_tensor(lo, w, hi.bitcast(F32), ALU.subtract).then_inc(w_lo, 1)
                if edge and t == 1:
                    dve.wait_ge(zeros_made, ZEROS)
                    dve.wait_ge(weights_in, 16 * WEIGHTS)
                    for ch in range(DC):
                        dve.tensor_scalar(wo_sb[:, ch, :], wo_raw[:, ch, :], mask_sb[:, ch:ch + 1], None, ALU.mult).then_inc(wo_masked, 1)
                for h in range(HEADS):
                    if h == 11 and b:
                        second_max_part(t - 1, 0)
                    if h == 1 and a:
                        wait(dve, xT_hi, t + 1)
                        wait(dve, v_ready, t)
                        dve.tensor_tensor(xT_2[1][:, :, :], g_bank[0][:, :].rearrange("p (c n) -> p c n", c=DC),
                                          xT_2[0][:, :, :].bitcast(F32), ALU.subtract).then_inc(xT_lo, 1)
                    if b:
                        n = HEADS * (t - 1) + h
                        half = h // 8
                        wait(dve, s_ready, n + 1)
                        wait(dve, max_turned, 2 * (t - 1) + half - 1)
                        at = (h % 8) * CH
                        dve.tensor_reduce(neg_max[half][:, at:at + CH], s_bank[h % 2][:, :].rearrange("p (c n) -> p c n", c=CH),
                                          AX.X, ALU.max, negate=True).then_inc(max_done, 1)
                    if h == 0 and e:
                        s = t - 4
                        wait(dve, h1_ready, s + 1)
                        wait(dve, xb_done, s + 1)
                        wait(dve, y_done, s)
                        dve.tensor_tensor(h1[:, :, :], g_bank[1][:, :].rearrange("p (c n) -> p c n", c=CH),
                                          xb[:, (turn - 4) % 3, :, :], ALU.add).then_inc(h1_done, 1)
                    if h == 2 and c:
                        second_max_part(t - 2, 1)
                    if h == 1 and e:
                        wait(dve, h1_done, t - 3)
                        statistics(h1[:, :, :], t - 4, stat2, CH, ln2_stats, 6 * (t + 1))
                    if h == 4 and e:
                        wait(dve, zT_ready, t - 4)
                        wait(dve, z_out, 16 * (t - 4))
                        norm(z, h1[:, :, :], t - 4, CH, ln2_stats, 6 * (t + 2), z_done)
                    if h == 7 and e:
                        wait(dve, zT_hi, t - 3)
                        wait(dve, lg_ready, t - 4)
                        dve.tensor_tensor(zT_2[1][:, :, :], g_bank[0][:, :].rearrange("p (c n) -> p c n", c=DC),
                                          zT_2[0][:, :, :].bitcast(F32), ALU.subtract).then_inc(zT_lo, 1)
                    if h == 6 and d:
                        s = t - 3
                        wait(dve, sums_in, 16 * (s + 1))
                        wait(dve, inv_out, 16 * s)
                        dve.reciprocal(inv_sums[:, :], sums[:, :]).then_inc(inv_done, 1)
                    for which in range(2):
                        if h == (5, 6)[which] and a:
                            rest(t, which)
                            wait(dve, rest_done[which], t + 1)
                            wait(dve, parts_out[which], 16 * t)
                            dve.tensor_copy(parts[:, which, 1, :, :], qk_rest[:, which, :, :]).then_inc(part1_done, 1)
                    if h == 8 and a:
                        wait(dve, v_ready, t + 1)
                        wait(dve, pv_ready, 4 * (t - 2))
                        for ch in range(CH):
                            ins = dve.tensor_tensor(v[:, turn, ch, :, 0:HD],
                                                    g_bank[1][:, ch * D:(ch + 1) * D].rearrange("p (h e) -> p h e", e=HD),
                                                    bv_sb[:, :].rearrange("p (h e) -> p h e", e=HD), ALU.add)
                        ins.then_inc(v_done, 1)
                    if h == 12 and e and turn == 1:
                        s = t - 4
                        waits_apart(dve, held, (lg_turned, s + 3))
                        have = range(2, 3) if edge and t == 4 else range(3)
                        for j in have:
                            for ch in range(CH):
                                ins = dve.max(top[:, j, ch, :], g_bank[0][:, ch * P + 32 * j:ch * P + 32 * j + EXPERTS])
                        ins.then_inc(top_done, 3)
                        j, n = have[0], len(have)
                        kept = bass.ds(CH * (s + 1 - n), CH * n)
                        dve.tensor_copy(logits[:, kept, :].rearrange("p (j c) e -> p j c e", c=CH),
                                        g_bank[0][:, 0:CH * P].rearrange("p (c j e) -> p j c e", c=CH, j=P // 32)[:, j:3, :, 0:EXPERTS]
                                        ).then_inc(lg_kept, 3)
                        wait(dve, top_done, s + 3)
                        dve.tensor_tensor(gap[:, kept].rearrange("p (j c) -> p j c", c=CH), top[:, j:3, :, 1], top[:, j:3, :, 0],
                                          ALU.subtract).then_inc(gap_done, 3)
                    if h == 10 and (not edge or t + 1 < SEQS):
                        norm_x_2(t + 1, (turn + 1) % 3)
                    if edge and t == 0 and h == 2:
                        norm_x_1(1, 1)
                    if h == 13 and (not edge or t + 2 < SEQS):
                        norm_x_1(t + 2, (turn + 2) % 3)
                    if h == 14 and e:
                        wait(dve, y_ready, t - 3)
                        wait(dve, out_out, 16 * (t - 4))
                        dve.tensor_tensor(o_sb[:, :, :], g_bank[0][:, :].rearrange("p (c n) -> p c n", c=CH), h1[:, :, :],
                                          ALU.add).then_inc(y_done, 1)
            norm_x_1(0, 0)
            for w, w_2 in ((wq_sb, wq_2), (wk_sb, wk_2), (wv_sb, wv_2)):
                dve.wait_ge(qkv_hi, 3)
                dve.tensor_tensor(w_2[1][:, :, :], w[:, :, :], w_2[0][:, :, :].bitcast(F32), ALU.subtract).then_inc(qkv_lo, 1)
            norm_x_2(0, 0)
            steps(dve, step)

            n = [0]

            def link(ins):
                n[0] += 1
                ins.then_inc(route, 1)
                dve.wait_ge(route, n[0])

            dve.wait_ge(route_exp, 1)
            link(dve.tensor_scalar(first_w[:, 1, :], first_w[:, 0, :], 1.0, None, ALU.add))
            link(dve.reciprocal(first_w[:, 2, :], first_w[:, 1, :]))
            link(dve.tensor_scalar(first_w[:, 3, :], first_w[:, 2, :], 1.0, None, ALU.is_ge))
            link(dve.tensor_reduce(any_p[:, 0:1], first_w[:, 3, :], AX.X, ALU.max))
            dve.wait_ge(flag_turned, 1)
            link(dve.tensor_reduce(flag_f[:, :], g_bank[0][0:1, 0:P], AX.X, ALU.max))
            dve.tensor_copy(flag_i[:, :], flag_f[:, :]).then_inc(flag_done, 1)

            dve.wait_ge(flag_done, 1)
            flag = dve.value_load(flag_i[0:1, 0:1], min_val=0, max_val=1)
            with dve.If(flag > 0):
                link(dve.tensor_reduce(best[:, :], logits[:, :, :], AX.X, ALU.max))
                link(dve.tensor_tensor(prob[:, :, :], logits[:, :, :],
                                       best[:, :].unsqueeze(2).broadcast_to([P, SEQS * CH, EXPERTS]), ALU.is_ge))
                link(dve.tensor_tensor(prob[:, :, :], prob[:, :, :],
                                       first_w[:, 3, :].unsqueeze(2).broadcast_to([P, SEQS * CH, EXPERTS]), ALU.mult))
                def route_one(s):
                    dve.wait_ge(e_o_in, s * 16 + 16)
                    for e in range(EXPERTS):
                        dve.wait_ge(e_y_ready, s * EXPERTS + (e + 1))
                        for ch in range(CH):
                            k = (s * EXPERTS + e) * CH + ch
                            if e:
                                dve.wait_ge(e_added, k - CH + 1)
                            dve.tensor_copy(weight[:, ch:ch + 1], prob[:, bass.ds(s * CH + ch, 1), e]).then_inc(route, 1)
                            dve.wait_ge(route, k + (ROUTE + 1))
                            dve.scalar_tensor_tensor(out=o_sb[:, ch, :], in0=g_bank[0][:, ch * D:(ch + 1) * D],
                                                     scalar=weight[:, ch:ch + 1], in1=o_sb[:, ch, :],
                                                     op0=ALU.mult, op1=ALU.add).then_inc(e_added, 1)

                each_sequence(dve, route_one)
            assert n[0] == ROUTE

        @block.tensor
        def _(pe):
            pe.wait_ge(consts_made, CONSTS)
            pe.wait_ge(qkv_lo, 3)

            def turn_tile(bank, src, last_sem):
                for dc in range(DC):
                    for ch in range(CH):
                        at = dc * TOK + ch * P
                        ins = pe.transpose(bank[:, at:at + P], src[:, ch, dc * P:(dc + 1) * P], ident[:, :])
                ins.then_inc(last_sem, 1)

            def product(out, left, right, chunks):
                passes = [(l, r, chunk) for l, r in ((0, 0), (1, 0), (0, 1)) for chunk in range(chunks)]
                for n, (l, r, chunk) in enumerate(passes):
                    ins = pe.matmul(out, left(l, chunk), right(r, chunk), start=(n == 0), stop=(n == len(passes) - 1))
                return ins

            def project_turned(out, w_2, src_2, m=0):
                return product(out, lambda i, dc: w_2[i][:, dc, m * P:(m + 1) * P], lambda i, dc: src_2[i][:, dc, :], DC)

            def project(bank, src_2, w_2, ch):
                return product(bank[:, ch * D:(ch + 1) * D], lambda i, dc: src_2[i][:, dc, ch * P:(ch + 1) * P],
                               lambda i, dc: w_2[i][:, dc, :], DC)

            def scores(s, h, turn):
                if h == 0:
                    for done in stacked:
                        wait(pe, done, 16 * len(PIECES) * (s + 1))
                wait(pe, max_done, HEADS * s + h - 1)
                for ch in range(CH):
                    ins = pe.matmul(s_bank[h % 2][:, ch * TOK:(ch + 1) * TOK],
                                    stack_q[turn][0:ROWS, h, ch * P:(ch + 1) * P], stack_k[turn][0:ROWS, h, :],
                                    start=True, stop=True)
                ins.then_inc(s_ready, 1)

            def scores_turned(s, h, turn):
                if h % 8 == 0:
                    wait(pe, max_in[h // 8], 16 * (s + 1))
                wait(pe, exp_done, HEADS * s + h - 1)
                for ch in range(CH):
                    ins = pe.matmul(t_bank[h % 2][:, ch * TOK:(ch + 1) * TOK],
                                    stack_k[turn][0:SROWS, h, ch * P:(ch + 1) * P], stack_q[turn][0:SROWS, h, :],
                                    start=True, stop=True)
                ins.then_inc(t_ready, 1)

            def attend(s, g, turn):
                wait(pe, exp_done, HEADS * s + GH * (g + 1))
                wait(pe, oT_done, 2 * s + g // 2 - 1)
                if g == 0:
                    wait(pe, v_done, s + 1)
                at = (g % 2) * TOK
                for ch in range(CH):
                    for i in range(GH):
                        h = GH * g + i
                        ins = pe.matmul(o_bank[g // 2][32 * i:32 * i + 32, at:at + TOK], v[:, turn, ch, h, :],
                                        probs[:, h % 8, ch, :], start=(ch == 0), stop=(ch == CH - 1),
                                        skip_group_check=True)
                ins.then_inc(pv_ready, 1)

            def turn_max(s, half):
                wait(pe, max_done, HEADS * s + 8 * (half + 1))
                pe.transpose(g_bank[1][:, 0:P], neg_max[half][:, :], ident[:, :]).then_inc(max_turned, 1)

            def step(t, turn, on, edge):
                a, b, c, d, e = on
                b0, b1 = g_bank
                if edge and t == 2:
                    pe.wait_ge(ones_made, 3)
                    pe.wait_ge(v_ones_made, 3)
                if edge and t == 3:
                    pe.wait_ge(w_lo, 4)
                for h in range(HEADS):
                    if b:
                        scores(t - 1, h, (turn - 1) % 3)
                    if h == 0:
                        wait(pe, y_done, t - 4)
                        if edge:
                            wait(pe, part0_done, 2 * DC * min(t, SEQS))
                        if a:
                            wait(pe, xn_done, CH * (t + 1))
                            turn_tile(b0, xn, xT_ready)
                    if c:
                        scores_turned(t - 2, h, (turn - 2) % 3)
                    if h == 1:
                        if d:
                            attend(t - 3, 3, turn)
                        wait(pe, h1_done, t - 3)
                        if edge:
                            wait(pe, max_lo, min(2 * t - 3, 2 * SEQS))
                            wait(pe, v_done, min(t, SEQS))
                        if c:
                            turn_max(t - 2, 1)
                    if h in (2, 3) and a:
                        wait(pe, xT_lo, t + 1)
                        ins = project_turned(b0[:, (h - 2) * TOK:(h - 1) * TOK], wq_2, xT_2, h - 2)
                        if h == 3:
                            ins.then_inc(q_ready, 1)
                    if h in (4, 5) and a:
                        if c:
                            wait(pe, max_lo, 2 * (t - 2) + 2)
                        ins = project_turned(b1[:, (h - 4) * TOK:(h - 3) * TOK], wk_2, xT_2, h - 4)
                        if h == 5:
                            ins.then_inc(k_ready, 1)
                    if h == 5 and e:
                        if a:
                            wait(pe, part0_done, 2 * DC * t + DC)
                        wait(pe, z_done, CH * (t - 3))
                        turn_tile(b0, z, zT_ready)
                    if h in (7, 8) and a:
                        wait(pe, part0_done, 2 * DC * (t + 1))
                        ins = project(b1, xT_2, wv_2, h - 7)
                        if h == 8:
                            ins.then_inc(v_ready, 1)
                    if h == 9 and e:
                        wait(pe, zT_lo, t - 3)
                        project_turned(b0[:, 0:TOK], ws1_2, zT_2).then_inc(hid_ready, 1)
                    if h == 10 and b:
                        if a:
                            wait(pe, v_done, t + 1)
                        elif c:
                            wait(pe, max_lo, 2 * (t - 2) + 2)
                        turn_max(t - 1, 0)
                    if h == 12 and e and turn == 1:
                        wait(pe, lg_done, t - 3)
                        for ch in range(CH):
                            ins = pe.transpose(b0[:, ch * P:(ch + 1) * P], lgT[:, ch * P:(ch + 1) * P], ident[:, :])
                        ins.then_inc(lg_turned, 3)
                    if h in (6, 10, 12) and c:
                        attend(t - 2, {6: 0, 10: 1, 12: 2}[h], (turn - 2) % 3)
                    if h == 11 and e:
                        wait(pe, relu_done, t - 3)
                        j = (turn + 1) % 3
                        project_turned(b0[:, 0:TOK], [w[:, j, :, :] for w in wr_2], zT_2).then_inc(lg_ready, 1)
                    if h == 13 and e:
                        if turn == 1:
                            wait(pe, lg_kept, t - 1)
                        else:
                            wait(pe, lg_done, t - 3)
                        wait(pe, hid_lo, t - 3)
                        for ch in range(CH):
                            ins = product(b0[:, ch * D:(ch + 1) * D], lambda i, _: hid_2[i][:, ch * P:(ch + 1) * P],
                                          lambda i, _: ws2_2[i][:, :], 1)
                        ins.then_inc(y_ready, 1)
                    if h in (14, 15) and d:
                        if b:
                            wait(pe, max_lo, 2 * (t - 1) + 1)
                        elif c:
                            wait(pe, max_lo, 2 * (t - 2) + 2)
                        wait(pe, o_lo, t - 2)
                        ins = project(b1, o_2, wo_2, h - 14)
                        if h == 15:
                            ins.then_inc(h1_ready, 1)

            steps(pe, step)
            pe.wait_ge(lg_kept, SEQS + 2)
            pe.wait_ge(route, 4)
            pe.transpose(g_bank[0][:, 0:P], any_p[:, :], ident[:, :]).then_inc(flag_turned, 1)

            pe.wait_ge(flag_done, 1)
            flag = pe.value_load(flag_i[0:1, 0:1], min_val=0, max_val=1)
            with pe.If(flag > 0):
                pe.wait_ge(e_w_in, 16 * (DC + 1))
                def route_one(s):
                    pe.wait_ge(e_z_in, s * 16 + 16)
                    wait(pe, e_added, s * (EXPERTS * CH))
                    turn_tile(g_bank[0], z, e_zT_ready)
                    pe.wait_ge(e_zT_done, s + 1)
                    for e in range(EXPERTS):
                        wait(pe, e_relu_done, s * EXPERTS + e)
                        for dc in range(DC):
                            ins = pe.matmul(g_bank[1][:, 0:TOK], w1_sb[:, dc, e, :], zT[:, dc, :],
                                            start=(dc == 0), stop=(dc == DC - 1))
                        ins.then_inc(e_hid_ready, 1)
                        pe.wait_ge(e_hid_done, s * EXPERTS + (e + 1))
                        wait(pe, e_added, (s * EXPERTS + e) * CH)
                        for ch in range(CH):
                            ins = pe.matmul(g_bank[0][:, ch * D:(ch + 1) * D], hid[:, ch * P:(ch + 1) * P], w2_sb[:, e, :],
                                            start=True, stop=True)
                        ins.then_inc(e_y_ready, 1)

                each_sequence(pe, route_one)

        @block.sync
        def _(sp):
            sp.wait_ge(flag_done, 1)
            flag = sp.value_load(flag_i[0:1, 0:1], min_val=0, max_val=1)
            with sp.If(flag > 0):
                for ch in range(DC):
                    sp.dma_start(w1_sb[:, ch, :, :], w1[:, ch * P:(ch + 1) * P, :].rearrange("e p f -> p e f")).then_inc(e_w_in, 16)
                sp.dma_start(w2_sb[:, :, :], w2.rearrange("e f n -> f e n")).then_inc(e_w_in, 16)
                def route_one(s):
                    wait(sp, e_zT_ready, s)
                    sp.dma_start(z[:, :, :], z_dram[bass.ds(s, 1), :, :].rearrange("o (c p) n -> p (o c) n", p=P)).then_inc(e_z_in, 16)
                    wait(sp, e_out, s * 16)
                    sp.dma_start(o_sb[:, :, :], out[bass.ds(s, 1), :, :].rearrange("o (c p) n -> p (o c) n", p=P)).then_inc(e_o_in, 16)
                    sp.wait_ge(e_added, (s + 1) * (EXPERTS * CH))
                    sp.dma_start(out[bass.ds(s, 1), :, :].rearrange("o (c p) n -> p (o c) n", p=P), o_sb[:, :, :]).then_inc(e_out, 16)

                each_sequence(sp, route_one)
                sp.wait_ge(e_out, SEQS * 16)


QKV = 6
WEIGHTS = 8
CONSTS = 3
ZEROS = 5
ROUTE = 8


_ORDER = ["ids", "emb", "wq", "bq", "wk", "bk", "wv", "bv", "wo", "bo", "mask", "ws1", "ws2", "w1", "w2", "wr"]


def kernel(x, L0_tok_embeddings, L0_attn_Wq, L0_attn_bq, L0_attn_Wk, L0_attn_bk, L0_attn_Wv, L0_attn_bv,
           L0_attn_Wo, L0_attn_bo, L0_attn_head_mask, L0_ffn_Ws1, L0_ffn_Ws2, L0_ffn_W1, L0_ffn_W2, L0_ffn_Wr):
    import numpy as np
    import concourse.bacc as bacc
    from concourse import mybir as mb
    from concourse.bass_utils import run_bass_kernel_spmd

    seqs, tok = x.shape
    d = L0_tok_embeddings.shape[1]
    heads = L0_attn_head_mask.shape[0]
    c = np.ascontiguousarray
    dims = np.arange(d)
    by_place = dims.reshape(heads, -1).T.reshape(-1)
    data = {
        "ids": c(np.asarray(x).reshape(-1, 128).T),
        "emb": c(np.asarray(L0_tok_embeddings)),
        "wq": c(np.asarray(L0_attn_Wq)[by_place].T), "wk": c(np.asarray(L0_attn_Wk)[by_place].T),
        "wv": c(np.asarray(L0_attn_Wv).T), "wo": c(np.asarray(L0_attn_Wo).T),
        "bq": c(np.asarray(L0_attn_bq)[by_place].reshape(-1, 128).T), "bk": c(np.asarray(L0_attn_bk)[by_place].reshape(-1, 128).T),
        "bv": c(np.asarray(L0_attn_bv)), "bo": c(np.asarray(L0_attn_bo)),
        "mask": c(np.repeat(np.asarray(L0_attn_head_mask), d // heads).reshape(-1, 128).T),
        "ws1": c(np.asarray(L0_ffn_Ws1)), "ws2": c(np.asarray(L0_ffn_Ws2)),
        "w1": c(np.asarray(L0_ffn_W1)), "w2": c(np.asarray(L0_ffn_W2)), "wr": c(np.asarray(L0_ffn_Wr)),
    }
    nc = bacc.Bacc("TRN2", target_bir_lowering=False, num_devices=1)
    arrays, args = {}, []
    for name in _ORDER:
        arrays[f"in_{name}"] = data[name]
        args.append(nc.dram_tensor(f"in_{name}", data[name].shape, mb.dt.from_np(data[name].dtype), kind="ExternalInput").ap())
    out = nc.dram_tensor("out_0", (seqs, tok, d), mb.dt.float32, kind="ExternalOutput").ap()
    tower(nc, *args, out)
    r = run_bass_kernel_spmd(nc, [arrays], core_ids=[0])
    return r.results[0]["out_0"]
```
